# Optimizing a Trainium2 kernel written in Bass

```python
import numpy as np
import jax
import jax.numpy as jnp

def _softmax(x, axis=-1):
    return jax.nn.softmax(x, axis=axis)

def _gelu(x):
    return jax.nn.gelu(x, approximate=True)

def _silu(x):
    return jax.nn.silu(x)

def _sigmoid(x):
    return jax.nn.sigmoid(x)

def _layernorm(x, axis=-1, eps=1e-05):
    m = jnp.mean(x, axis=axis, keepdims=True)
    v = jnp.var(x, axis=axis, keepdims=True)
    return (x - m) / jnp.sqrt(v + eps)

def _scatter_add(tgt, idx, src, axis=0):
    return tgt.at[idx].add(src)

def _segment_sum(src, seg, n):
    return jax.ops.segment_sum(src, seg, n)
kernel_name = 'mk_xattn_seq_d1_seqx_r2_996935'

def setup_inputs(seed: int=0):
    np.random.seed(seed)
    _w = jnp.asarray

    def _rec_inputs():
        import jax
        import jax.numpy as jnp
        _rk = jax.random.key(seed)
        x = 7.22e-05 + 1 * jax.random.normal(jax.random.fold_in(_rk, 1), (1, 4096, 512), jnp.float32)
        _lenS = 4096 - jax.random.randint(jax.random.fold_in(_rk, 7), (1,), 0, max(1, 4096 // 4) + 1, jnp.int32)
        _lenS2 = 3202 - jax.random.randint(jax.random.fold_in(_rk, 8), (1,), 0, max(1, 3202 // 4) + 1, jnp.int32)
        _ctx_1024P = jax.random.normal(jax.random.fold_in(_rk, 11), (1, 16, 512), jnp.float32)
        _ctx_1024c = jax.random.dirichlet(jax.random.fold_in(_rk, 511), 0.3 * jnp.ones((16,), jnp.float32), (1, 3202))
        _ctx_1024t = jnp.einsum('bsk,bkd->bsd', _ctx_1024c, _ctx_1024P)
        _ctx_1024t = _ctx_1024t * jax.lax.rsqrt(jnp.mean(jnp.square(_ctx_1024t)) + 1e-12) * 0.953939
        ctx_1024 = 4.13588e-05 + 0.999923 * (_ctx_1024t + 0.3 * jax.random.normal(jax.random.fold_in(_rk, 611), (1, 3202, 512), jnp.float32))
        itok_BxS2_4_31999 = jax.random.randint(jax.random.fold_in(_rk, 12), (1, 3202), 4, 16000, jnp.int32)
        _ctxb_2048x64P = jax.random.normal(jax.random.fold_in(_rk, 13), (1, 16, 64), jnp.float32)
        _ctxb_2048x64c = jax.random.dirichlet(jax.random.fold_in(_rk, 513), 0.3 * jnp.ones((16,), jnp.float32), (1, 3202))
        _ctxb_2048x64t = jnp.einsum('bsk,bkd->bsd', _ctxb_2048x64c, _ctxb_2048x64P)
        _ctxb_2048x64t = _ctxb_2048x64t * jax.lax.rsqrt(jnp.mean(jnp.square(_ctxb_2048x64t)) + 1e-12) * 0.953939
        ctxb_2048x64 = 0.50053 + 0.288505 * (_ctxb_2048x64t + 0.3 * jax.random.normal(jax.random.fold_in(_rk, 613), (1, 3202, 64), jnp.float32))
        return (x, ctx_1024, itok_BxS2_4_31999, ctxb_2048x64)
    x, ctx_1024, itok_BxS2_4_31999, ctxb_2048x64 = _rec_inputs()

    def _L0_xattn_setup():
        import jax, jax.numpy as jnp
        import numpy as np
        BATCH, T, H, S, P, NH = (4, 1024, 512, 64, 64, 8)
        HD = H // NH

        def _layernorm(x, g, b):
            mu = jnp.mean(x, axis=-1, keepdims=True)
            var = jnp.mean((x - mu) ** 2, axis=-1, keepdims=True)
            return (x - mu) * jax.lax.rsqrt(var + 1e-05) * g + b

        def _mha(q_in, kv_in, W_qkv, b_qkv, W_o, b_o):
            Wq, Wk, Wv = jnp.split(W_qkv, 3, axis=0)
            bq, bk, bv = jnp.split(b_qkv, 3, axis=0)

            def heads(x, W, b):
                y = x @ W.T + b
                return y.reshape(y.shape[0], y.shape[1], NH, HD).transpose(0, 2, 1, 3)
            q, k, v = (heads(q_in, Wq, bq), heads(kv_in, Wk, bk), heads(kv_in, Wv, bv))
            scores = jnp.einsum('bhqd,bhkd->bhqk', q, k) * (1.0 / np.sqrt(HD))
            attn = jax.nn.softmax(scores, axis=-1)
            out = jnp.einsum('bhqk,bhkd->bhqd', attn, v)
            out = out.transpose(0, 2, 1, 3).reshape(q_in.shape)
            return out @ W_o.T + b_o
        key = jax.random.key(seed)
        ks = jax.random.split(key, 16)
        sH = 1.0 / np.sqrt(H)
        d = {}
        d['builder_state'] = jax.random.normal(ks[0], (BATCH, T, H), jnp.float32)
        d['base_state'] = jax.random.normal(ks[1], (BATCH, T, H), jnp.float32)
        d['input_ids'] = jax.random.randint(ks[2], (BATCH, T), 0, 16000)
        d['program_probs'] = jax.random.uniform(ks[3], (BATCH, T, P), jnp.float32)
        d['A'] = jax.random.normal(ks[4], (S, S), jnp.float32) * (0.5 / np.sqrt(S))
        d['Bmat'] = jax.random.normal(ks[5], (H, S), jnp.float32) * sH
        d['Cmat'] = jax.random.normal(ks[6], (S, H), jnp.float32) * (1.0 / np.sqrt(S))
        d['W_in'] = jax.random.normal(ks[7], (H, H), jnp.float32) * sH
        d['b_in'] = jnp.zeros((H,), jnp.float32)
        d['W_qkv'] = jax.random.normal(ks[8], (3 * H, H), jnp.float32) * sH
        d['b_qkv'] = jnp.zeros((3 * H,), jnp.float32)
        d['W_o'] = jax.random.normal(ks[9], (H, H), jnp.float32) * sH
        d['b_o'] = jnp.zeros((H,), jnp.float32)
        d['W_prog'] = jax.random.normal(ks[10], (H, P), jnp.float32) * (1.0 / np.sqrt(P))
        d['b_prog'] = jnp.zeros((H,), jnp.float32)
        d['g1'] = jnp.ones((H,), jnp.float32)
        d['beta1'] = jnp.zeros((H,), jnp.float32)
        d['g2'] = jnp.ones((H,), jnp.float32)
        d['beta2'] = jnp.zeros((H,), jnp.float32)
        return d
    _L0_xattn_all = _L0_xattn_setup()
    _L0_xattn_in = {k: v for k, v in _L0_xattn_all.items() if k in ('A', 'Bmat', 'Cmat', 'W_in', 'b_in', 'W_qkv', 'b_qkv', 'W_o', 'b_o', 'W_prog', 'b_prog', 'g1', 'beta1', 'g2', 'beta2')}
    del _L0_xattn_all
    return {'x': x, 'ctx_1024': ctx_1024, 'itok_BxS2_4_31999': itok_BxS2_4_31999, 'ctxb_2048x64': ctxb_2048x64, 'L0_xattn_A': _L0_xattn_in['A'], 'L0_xattn_Bmat': _L0_xattn_in['Bmat'], 'L0_xattn_Cmat': _L0_xattn_in['Cmat'], 'L0_xattn_W_in': _L0_xattn_in['W_in'], 'L0_xattn_b_in': _L0_xattn_in['b_in'], 'L0_xattn_W_qkv': _L0_xattn_in['W_qkv'], 'L0_xattn_b_qkv': _L0_xattn_in['b_qkv'], 'L0_xattn_W_o': _L0_xattn_in['W_o'], 'L0_xattn_b_o': _L0_xattn_in['b_o'], 'L0_xattn_W_prog': _L0_xattn_in['W_prog'], 'L0_xattn_b_prog': _L0_xattn_in['b_prog'], 'L0_xattn_g1': _L0_xattn_in['g1'], 'L0_xattn_beta1': _L0_xattn_in['beta1'], 'L0_xattn_g2': _L0_xattn_in['g2'], 'L0_xattn_beta2': _L0_xattn_in['beta2']}

def reference(x, ctx_1024, itok_BxS2_4_31999, ctxb_2048x64, L0_xattn_A, L0_xattn_Bmat, L0_xattn_Cmat, L0_xattn_W_in, L0_xattn_b_in, L0_xattn_W_qkv, L0_xattn_b_qkv, L0_xattn_W_o, L0_xattn_b_o, L0_xattn_W_prog, L0_xattn_b_prog, L0_xattn_g1, L0_xattn_beta1, L0_xattn_g2, L0_xattn_beta2):
    import jax
    import jax.numpy as jnp

    def _L0_xattn_ref(builder_state, base_state, input_ids, program_probs, A, Bmat, Cmat, W_in, b_in, W_qkv, b_qkv, W_o, b_o, W_prog, b_prog, g1, beta1, g2, beta2):
        import jax, jax.numpy as jnp
        import numpy as np
        BATCH, T, H, S, P, NH = (4, 1024, 512, 64, 64, 8)
        HD = H // NH

        def _layernorm(x, g, b):
            mu = jnp.mean(x, axis=-1, keepdims=True)
            var = jnp.mean((x - mu) ** 2, axis=-1, keepdims=True)
            return (x - mu) * jax.lax.rsqrt(var + 1e-05) * g + b

        def _mha(q_in, kv_in, W_qkv, b_qkv, W_o, b_o):
            Wq, Wk, Wv = jnp.split(W_qkv, 3, axis=0)
            bq, bk, bv = jnp.split(b_qkv, 3, axis=0)

            def heads(x, W, b):
                y = x @ W.T + b
                return y.reshape(y.shape[0], y.shape[1], NH, HD).transpose(0, 2, 1, 3)
            q, k, v = (heads(q_in, Wq, bq), heads(kv_in, Wk, bk), heads(kv_in, Wv, bv))
            scores = jnp.einsum('bhqd,bhkd->bhqk', q, k) * (1.0 / np.sqrt(HD))
            attn = jax.nn.softmax(scores, axis=-1)
            out = jnp.einsum('bhqk,bhkd->bhqd', attn, v)
            out = out.transpose(0, 2, 1, 3).reshape(q_in.shape)
            return out @ W_o.T + b_o
        residual = builder_state
        x = _layernorm(builder_state, g1, beta1)
        base_n = _layernorm(base_state, g1, beta1)
        x = residual + _mha(x, base_n, W_qkv, b_qkv, W_o, b_o)
        residual = x
        xn = _layernorm(x, g2, beta2)
        U = (xn @ W_in.T + b_in) @ Bmat

        def step(s, u_t):
            s = jax.nn.silu(s @ A.T) + u_t
            return (s, s)
        _, states = jax.lax.scan(step, jnp.zeros((builder_state.shape[0], S), U.dtype), U.transpose(1, 0, 2))
        ssm_out = jnp.einsum('tbs,sh->bth', states, Cmat)
        x = residual + ssm_out
        mod = program_probs.mean(axis=1) @ W_prog.T + b_prog
        return x + mod[:, None, :]
    x = _L0_xattn_ref(x, ctx_1024, itok_BxS2_4_31999, ctxb_2048x64, L0_xattn_A, L0_xattn_Bmat, L0_xattn_Cmat, L0_xattn_W_in, L0_xattn_b_in, L0_xattn_W_qkv, L0_xattn_b_qkv, L0_xattn_W_o, L0_xattn_b_o, L0_xattn_W_prog, L0_xattn_b_prog, L0_xattn_g1, L0_xattn_beta1, L0_xattn_g2, L0_xattn_beta2)
    return x

_drawn_inputs = setup_inputs


def setup_inputs(seed=0):
    import zlib

    import numpy as np

    out = dict(_drawn_inputs(seed))
    spreads = {'L0_xattn_b_in': (0.0, 0.1),
     'L0_xattn_b_qkv': (0.0, 0.1),
     'L0_xattn_b_o': (0.0, 0.1),
     'L0_xattn_b_prog': (0.0, 0.1),
     'L0_xattn_g1': (1.0, 0.2),
     'L0_xattn_beta1': (0.0, 0.1),
     'L0_xattn_g2': (1.0, 0.2),
     'L0_xattn_beta2': (0.0, 0.1)}
    factors = {}
    for name, (base, spread) in spreads.items():
        noise = np.random.default_rng([zlib.crc32(name.encode()), seed]).standard_normal(out[name].shape)
        drawn = base * np.exp(spread * noise) if base else spread * noise
        out[name] = jnp.asarray(drawn.astype(out[name].dtype))
    for name, factor in factors.items():
        out[name] = (out[name] * factor).astype(out[name].dtype)
    return out
```

```python
from contextlib import ExitStack

import concourse.bass as bass
from concourse import mybir

F32 = mybir.dt.float32
F32R = mybir.dt.float32r
I32 = mybir.dt.int32
ALU = mybir.AluOpType
ACT = mybir.ActivationFunctionType
AX_X = mybir.AxisListType.X

P = 128
T = 4096
KEYS = 3202
KT_TILES = -(-KEYS // P)
KPAD = KT_TILES * P
H = 512
FC = H // P
NH = 8
HD = H // NH
SD = 64
EPS = 1e-5
SCALE = HD ** -0.5

GT = 2
GW = GT * P
CTX_G = KPAD // GW
X_G = T // GW
NG = CTX_G + X_G

QB = 512
QT_N = QB // P
PAIRS = NH // 2
ITERS = (T // QB) * PAIRS
UNITS = 2 * QT_N
CHUNKS = [(0, 1024), (1024, 1024), (2048, 1024), (3072, KEYS - 3072)]
NC = len(CHUNKS)
GROUPS = [range(g, min(g + 4, KT_TILES)) for g in range(0, KT_TILES, 4)]
NGR = len(GROUPS)
EXP_SPLIT = 12 * P
LO_SPLIT = 1602

LCH = 16
NCH = T // LCH
TOL2 = 2.0 ** -38

LN_STEPS = 14


def wait(eng, sem, value):
    if not (isinstance(value, int) and value <= 0):
        eng.wait_ge(sem, value)


def wait_apart(eng, sem, value, tick):
    wait(eng, sem, value)
    if not isinstance(value, int):
        eng.sem_inc(tick, 1)


def build(nc, x, ctx, ctxb, w_qkv_t, w_o_t, w_in, bmat, w_prog_t, a_t, cmat, cols, bv_rows, bo_rows,
          b_prog, out):
    es = ExitStack()
    with es:
        def sb(name, shape, dt=F32):
            return es.enter_context(nc.sbuf_tensor(name, shape, dt))

        def sem(name):
            return es.enter_context(nc.semaphore(name))

        q_scratch = nc.dram_tensor("q_scratch", [ITERS, P, QB], F32).ap()
        o_scratch = nc.dram_tensor("o_scratch", [ITERS, 2, P, QT_N * HD], F32).ap()

        kt = sb("kt", [P, FC * KPAD])
        big = sb("big", [P, KT_TILES * H + 2 * KPAD])
        k_split = sb("k_split", [P, 2, KEYS], F32R)
        q_split = sb("q_split", [P, 2, 2, QB], F32R)
        work = sb("work", [P, 4096])
        wo_qo = sb("wo_qo", [P, FC, H])
        qt_sb = sb("qt_sb", [P, QB])
        pt_sb = sb("pt_sb", [P, 2, QB])
        o_half = sb("o_half", [P, 2, P])
        o_out = sb("o_out", [P, 2, QT_N, HD])
        w_u = sb("w_u", [P, FC, SD])
        ident = sb("ident", [P, P])
        fold = sb("fold", [P, HD])
        ones = sb("ones", [P, 1])
        zeros = sb("zeros", [P, NC])
        col = sb("col", [P, 7, FC])
        bv = sb("bv", [P, H])
        bo = sb("bo", [P, H])
        c_aug = sb("c_aug", [SD + 1, H])
        bp = sb("bp", [1, H])
        at = sb("at", [SD, SD])
        cu = sb("cu", [SD, 1])
        mean = sb("mean", [SD, 1])
        stats = sb("stats", [P, GT, 6])
        mv = sb("mv", [P, GT, 2])
        ve = sb("ve", [P, GT])
        yi = sb("yi", [P, GT], I32)
        ya = sb("ya", [P, GT])
        yb = sb("yb", [P, GT])
        mx = sb("mx", [P, 4, NC])
        mxn = sb("mxn", [P, 4, NC])
        negm = sb("negm", [P, 4])
        den = sb("den", [P, 4, 2])
        dsum = sb("dsum", [P, 4])
        rden = sb("rden", [P, 4])
        flag_f = sb("flag_f", [1, 2])
        flag = sb("flag", [1, 1], I32)
        ps = es.enter_context(nc.psum_tensor("ps", [P, 8, 512], F32))

        g1, be1, g2, be2, bq, bk, bin_ = (col[:, i, :] for i in range(7))
        kt4 = kt[:, :].rearrange("p (c k) -> p c k", c=FC)
        v = big[:, 0:KT_TILES * H].rearrange("p (t f) -> p t f", t=KT_TILES)
        prow = big[:, KT_TILES * H:].rearrange("p (s k) -> p s k", s=2)
        w3 = big[:, KT_TILES * H:KT_TILES * H + 3 * FC * H].rearrange("p (w c n) -> p w c n", w=3, c=FC)
        win_sb = v[:, 22:26, :]
        b_sb = v[:, 21, 0:FC * SD].rearrange("p (c s) -> p c s", c=FC)
        cb_sb = big[:, 17 * H:17 * H + KT_TILES * SD].rearrange("p (t s) -> p t s", t=KT_TILES)
        wp_sb = v[0:SD, 16, :]
        xs = work[:, 0:1024].rearrange("p (t f) -> p t f", t=GT)
        og = work[:, 0:1024].rearrange("p (t h d) -> p t h d", t=GT, h=NH)
        xn = work[:, 1024:2048].rearrange("p (t f) -> p t f", t=GT)
        nt = work[:, 2048:4096].rearrange("p (s c k) -> p s c k", s=2, c=FC)
        v_head = work[:, 0:2 * KT_TILES * HD].rearrange("p (s t d) -> p s t d", s=2, t=KT_TILES)
        u_all = kt[0:SD, 0:T]
        s_all = kt[0:SD + 1, T:2 * T]
        ot = kt[:, 2 * T:2 * T + 2048].rearrange("p (s c k) -> p s c k", s=2, c=FC)
        xb = kt[:, 2 * T + 2048:2 * T + 4096].rearrange("p (s t f) -> p s t f", s=2, t=GT)
        x1 = big[:, 0:(T // P) * H].rearrange("p (t f) -> p t f", t=T // P)
        st = work[0:SD, 0:2 * NCH].rearrange("p (s c) -> p s c", s=2)
        sg = work[0:SD, 512:512 + 2 * NCH].rearrange("p (s c) -> p s c", s=2)
        end1 = work[0:SD, 1024:1024 + NCH]
        diff = work[0:SD, 1280:1280 + NCH]
        sq = work[0:SD, 1536:1536 + 2 * NCH].rearrange("p (s c) -> p s c", s=2)
        lhs_row = work[0:1, 2048:2048 + NCH]
        ok_row = work[0:1, 2304:2304 + NCH]
        e_row = work[0:1, 2560:2560 + NCH]
        stage = work[0:SD + 1, 3072:3584].rearrange("p (s k) -> p s k", s=2)
        u_steps = u_all.rearrange("p (c k) -> p k c", k=LCH)
        s_steps = s_all[0:SD, :].rearrange("p (c k) -> p k c", k=LCH)

        setup_loaded = sem("setup_loaded"); w_loaded = sem("w_loaded"); wo_loaded = sem("wo_loaded")
        consts = sem("consts"); setup_mm = sem("setup_mm"); setup_ev = sem("setup_ev")
        ln_step = sem("ln_step")
        tick = sem("tick")
        xs_loaded = sem("xs_loaded"); normed = sem("normed"); transposed = sem("transposed")
        nt_ready = sem("nt_ready"); kq_done = sem("kq_done"); kq_evac = sem("kq_evac")
        v_done = sem("v_done"); v_evac = sem("v_evac"); q_stored = sem("q_stored")
        p_padded = sem("p_padded"); qt_loaded = sem("qt_loaded")
        k_hi = sem("k_hi"); q_hi = sem("q_hi"); even_ready = sem("even_ready"); odd_ready = sem("odd_ready")
        qt_used = sem("qt_used"); vh_even = sem("vh_even"); vh_odd = sem("vh_odd")
        scored = sem("scored"); max_part = sem("max_part"); neg_max = sem("neg_max")
        exped = sem("exped"); turned = sem("turned"); pt_ready = sem("pt_ready"); pv_done = sem("pv_done")
        den_sum = sem("den_sum"); rden_ready = sem("rden_ready"); half_ready = sem("half_ready")
        folded = sem("folded"); o_scaled = sem("o_scaled")
        o_even_stored = sem("o_even_stored"); o_odd_stored = sem("o_odd_stored")
        og_loaded = sem("og_loaded"); x2_loaded = [sem("x2_loaded_0"), sem("x2_loaded_1")]; xb_ready = sem("xb_ready")
        o_turned = sem("o_turned"); ot_ready = sem("ot_ready"); y_done = sem("y_done")
        x1_ready = sem("x1_ready"); normed2 = sem("normed2"); n2_turned = sem("n2_turned")
        n2t_ready = sem("n2t_ready"); u_done = sem("u_done"); u_ready = sem("u_ready")
        z_done = sem("z_done"); silu_done = sem("silu_done"); st_ready = sem("st_ready")
        saved = sem("saved"); cmp_step = sem("cmp_step"); sums_done = sem("sums_done")
        flag_ready = sem("flag_ready")
        seq_z = sem("seq_z"); seq_silu = sem("seq_silu"); seq_st = sem("seq_st"); seq_saved = sem("seq_saved")
        staged = sem("staged"); f_done = sem("f_done"); f_added = sem("f_added"); stored = sem("stored")

        block = es.enter_context(nc.Block())

        def b_steps(eng, front, back):
            front(0, 0)
            for g in (0, 1):
                front(g + 1, (g + 1) % 2)
                back(g, g % 2)
            with eng.Fori(0, 5) as i:
                for s in (0, 1):
                    front(2 * i + (3 + s), (1 + s) % 2)
                    back(2 * i + (2 + s), s)
            for g in (12, 13, 14):
                front(g + 1, (g + 1) % 2)
                back(g, g % 2)
            with eng.Fori(0, 6) as i:
                for s in (0, 1):
                    front(2 * i + (16 + s), s)
                    back(2 * i + (15 + s), 1 - s, i + 1, s)
            front(NG - 1, (NG - 1) % 2)
            back(NG - 2, (NG - 2) % 2)
            back(NG - 1, (NG - 1) % 2)

        def x_group(g, block_half):
            return block_half or ((g - CTX_G) // 2, (g - CTX_G) % 2)

        def d_steps(eng, front, back):
            front(0, 0)
            for d in (0, 1):
                front(d + 1, (d + 1) % 2)
                back(d, d % 2)
            with eng.Fori(0, 6) as i:
                for s in (0, 1):
                    front(2 * i + (3 + s), (1 + s) % 2)
                    back(2 * i + (2 + s), s)
            front(X_G - 1, (X_G - 1) % 2)
            back(X_G - 2, (X_G - 2) % 2)
            back(X_G - 1, (X_G - 1) % 2)

        def c_steps(eng, body):
            body(0, first=True)
            with eng.Fori(1, ITERS - 1) as it:
                body(it)
            body(ITERS - 1, last=True)

        @block.sync
        def _(sp):
            for dst, src in ((b_sb, bmat), (win_sb, w_in), (cb_sb, ctxb), (wp_sb, w_prog_t),
                             (col[:, :, :], cols), (bp[:, :], b_prog), (at[:, :], a_t),
                             (c_aug[0:SD, :], cmat), (bv[:, :], bv_rows), (bo[:, :], bo_rows)):
                sp.dma_start(dst, src).then_inc(setup_loaded, 16)

            def load_ctx(g):
                wait(sp, normed, g)
                sp.dma_start(xs, ctx.rearrange("(g t p) f -> g p t f", p=P, t=GT)[g]).then_inc(xs_loaded, 16)

            def load_x(h):
                wait(sp, normed, h + CTX_G)
                sp.dma_start(xs, x.rearrange("(g t p) f -> g p t f", p=P, t=GT)[h]).then_inc(xs_loaded, 16)

            def store_q(h, blk, half):
                wait(sp, kq_evac, FC * (h + CTX_G + 1))
                dst = q_scratch.rearrange("(b c) p k -> b p c k", c=FC)[blk]
                sp.dma_start(dst[:, :, half * GW:(half + 1) * GW],
                             wo_qo[:, :, half * GW:(half + 1) * GW]).then_inc(q_stored, 16)

            load_ctx(0)
            sp.dma_start(w3, w_qkv_t).then_inc(w_loaded, 16)
            load_ctx(1)
            with sp.Fori(2, CTX_G) as g:
                load_ctx(g)
            load_x(0)
            load_x(1)
            with sp.Fori(0, X_G // 2 - 1) as i:
                for s in (0, 1):
                    store_q(2 * i + s, i, s)
                    load_x(2 * i + (2 + s))
            for s in (0, 1):
                store_q(X_G - 2 + s, X_G // 2 - 1, s)
            sp.wait_ge(q_stored, 16 * X_G)
            sp.dma_start(qt_sb[:, :], q_scratch[0]).then_inc(qt_loaded, 16)
            sp.dma_start(wo_qo[:, :, :], w_o_t).then_inc(wo_loaded, 16)

            def store_odd(it):
                sp.wait_ge(o_scaled, UNITS * it + UNITS)
                sp.dma_start(o_scratch[it, 1], o_out[:, 1, :, :].rearrange("p q d -> p (q d)"))\
                    .then_inc(o_odd_stored, 16)

            def c_body(it, first=False, last=False):
                if not first:
                    store_odd(it - 1)
                if not last:
                    sp.wait_ge(qt_used, it + 1)
                    sp.dma_start(qt_sb[:, :], q_scratch[it + 1]).then_inc(qt_loaded, 16)
                sp.wait_ge(o_scaled, UNITS * it + QT_N)
                sp.dma_start(o_scratch[it, 0], o_out[:, 0, :, :].rearrange("p q d -> p (q d)"))\
                    .then_inc(o_even_stored, 16)

            c_steps(sp, c_body)
            store_odd(ITERS - 1)
            sp.wait_ge(o_even_stored, 16 * ITERS)
            sp.wait_ge(o_odd_stored, 16 * ITERS)

            def d_load(d, blk, half):
                wait(sp, o_turned, 2 * d)
                src = o_scratch.rearrange("(b c) h p k -> b p (c h) k", c=FC)[blk]
                for t in range(GT):
                    q = half * GT + t
                    sp.dma_start(og[:, t], src[:, :, q * HD:(q + 1) * HD]).then_inc(og_loaded, 16)
                wait(sp, x1_ready, GT * (d - 1))
                sp.dma_start(xb[:, half], x.rearrange("(g t p) f -> g p t f", p=P, t=GT)[d])\
                    .then_inc(x2_loaded[half], 16)

            for s in (0, 1):
                d_load(s, 0, s)
            with sp.Fori(1, X_G // 2) as i:
                for s in (0, 1):
                    d_load(2 * i + s, i, s)

            def f_store(d):
                sp.wait_ge(f_added, GT * (d + 1))
                sp.dma_start(out.rearrange("(g t p) f -> g p t f", p=P, t=GT)[d],
                             x1[:, bass.ds(GT * d, GT), :]).then_inc(stored, 16)

            with sp.Fori(0, X_G) as d:
                f_store(d)
            sp.wait_ge(stored, 16 * X_G)

        @block.gpsimd
        def _(pool):
            nc.gpsimd.memset(ident[:, :], 0.0).then_inc(consts, 1)
            nc.gpsimd.memset(fold[:, :], 0.0).then_inc(consts, 1)
            nc.gpsimd.memset(ones[:, :], 1.0).then_inc(consts, 1)
            nc.gpsimd.memset(zeros[:, :], 0.0).then_inc(consts, 1)
            pool.wait_ge(consts, 4)
            nc.gpsimd.affine_select(out=ident[:, :], in_=ident[:, :], compare_op=ALU.not_equal, fill=1.0,
                                    base=0, pattern=[[-1, P]], channel_multiplier=1).then_inc(consts, 1)
            nc.gpsimd.affine_select(out=fold[:, :], in_=fold[:, :], compare_op=ALU.not_equal, fill=1.0,
                                    base=0, pattern=[[-1, HD]], channel_multiplier=1).then_inc(consts, 1)
            pool.wait_ge(consts, 6)
            nc.gpsimd.affine_select(out=fold[:, :], in_=fold[:, :], compare_op=ALU.not_equal, fill=1.0,
                                    base=-HD, pattern=[[-1, HD]], channel_multiplier=1).then_inc(consts, 1)

            pool.wait_ge(kq_done, FC * NG)
            pool.wait_ge(v_evac, GT * CTX_G)
            nc.gpsimd.memset(prow[:, :, KEYS:KPAD], 0.0).then_inc(p_padded, 1)

            def v_copy(slot, pr, done):
                vv = v.rearrange("p t (c s d) -> p c s t d", c=FC, s=2)
                nc.gpsimd.tensor_copy(v_head[:, slot], vv[:, pr, slot]).then_inc(done, 1)

            v_copy(0, 0, vh_even)

            def c_body(it, first=False, last=False):
                wait(pool, pv_done, NGR * UNITS * it)
                v_copy(1, it % PAIRS, vh_odd)
                if not last:
                    pool.wait_ge(pv_done, NGR * (UNITS * it + QT_N))
                    v_copy(0, (it + 1) % PAIRS, vh_even)

            c_steps(pool, c_body)

            def d_body(i, slot):
                pool.wait_ge(x2_loaded[slot], 16 * (i + 1))
                for t in range(GT):
                    ins = nc.gpsimd.tensor_tensor(xb[:, slot, t], xb[:, slot, t], bo[:, :], ALU.add)
                ins.then_inc(xb_ready, 1)

            with pool.Fori(0, X_G // 2) as i:
                for s in (0, 1):
                    d_body(i, s)

        @block.scalar
        def _(act):
            def b_front(g, slot):
                wait(act, kq_done, FC * (g - 1))
                for c in range(FC):
                    if c % 2 == 0:
                        act.wait_ge(transposed, 2 * g + (c // 2 + 1))
                    nc.scalar.activation(nt[:, slot, c], ps[:, c // 2, (c % 2) * GW:(c % 2 + 1) * GW],
                                         ACT.Identity, bias=be1[:, c:c + 1], scale=g1[:, c:c + 1])\
                        .then_inc(nt_ready, 1)

            def b_back(g, slot, *block_half):
                is_ctx = isinstance(g, int) and g < CTX_G or not isinstance(g, int) and not block_half
                if not is_ctx:
                    blk, half = x_group(g, block_half)
                    wait(act, q_stored, 16 * ((g - CTX_G) - 1))
                for c in range(FC):
                    act.wait_ge(kq_done, FC * g + (c + 1))
                    if is_ctx:
                        dst = kt4[:, c, bass.ds(g * GW, GW)]
                    else:
                        dst = wo_qo[:, c, half * GW:(half + 1) * GW]
                    nc.scalar.activation(dst, ps[:, 2 + c, 0:GW], ACT.Identity,
                                         bias=(bk if is_ctx else bq)[:, c:c + 1]).then_inc(kq_evac, 1)

            act.wait_ge(setup_loaded, 16 * 10)
            b_steps(act, b_front, b_back)

            def exp_part(u, slot, s4, part):
                a, b = ((0, EXP_SPLIT), (EXP_SPLIT, KEYS))[part]
                nc.scalar.activation(prow[:, slot, a:b], prow[:, slot, a:b], ACT.Exp,
                                     bias=negm[:, s4:s4 + 1], accum_out=den[:, s4, part:part + 1])\
                    .then_inc(exped, 1)

            def exp_begin(u, s4):
                act.wait_ge(neg_max, u + 1)
                wait(act, rden_ready, u - 3)

            def evac(u, g):
                G = NGR * u + g
                act.wait_ge(turned, G + 1)
                wait(act, pv_done, G - 1)
                n = len(GROUPS[g]) * P
                b = (pt_slot0 + g) % 2
                nc.scalar.activation(pt_sb[:, b, 0:n], ps[:, 4 + b, 0:n], ACT.Copy).then_inc(pt_ready, 1)

            exp_begin(0, 0)
            for part in (0, 1):
                exp_part(0, 0, 0, part)

            def c_body(it, first=False, last=False):
                nonlocal pt_slot0
                for j in range(UNITS):
                    u = UNITS * it + j
                    pt_slot0 = (NGR * j) % 2
                    more = not (last and j == UNITS - 1)
                    s4 = (j + 1) % 4
                    evac(u, 0)
                    evac(u, 1)
                    if more:
                        exp_begin(u + 1, s4)
                        exp_part(u + 1, (j + 1) % 2, s4, 0)
                    evac(u, 2)
                    evac(u, 3)
                    if more:
                        exp_part(u + 1, (j + 1) % 2, s4, 1)
                    for g in range(4, NGR):
                        evac(u, g)

            pt_slot0 = 0
            c_steps(act, c_body)

            def d_front(d, slot):
                wait(act, y_done, GT * (d - 1))
                for k in range(2):
                    act.wait_ge(o_turned, 2 * d + (k + 1))
                    nc.scalar.activation(ot[:, slot, 2 * k:2 * k + 2].rearrange("p c k -> p (c k)"),
                                         ps[:, k, :], ACT.Copy).then_inc(ot_ready, 1)

            def d_back(d, slot):
                wait(act, u_done, d - 1)
                for c in range(FC):
                    if c % 2 == 0:
                        act.wait_ge(n2_turned, 2 * d + (c // 2 + 1))
                    nc.scalar.activation(nt[:, slot, c], ps[:, 4 + c // 2, (c % 2) * GW:(c % 2 + 1) * GW],
                                         ACT.Identity, bias=be2[:, c:c + 1], scale=g2[:, c:c + 1])\
                        .then_inc(n2t_ready, 1)
                act.wait_ge(u_done, d + 1)
                nc.scalar.activation(u_all[:, bass.ds(d * GW, GW)], ps[0:SD, 6, 0:GW], ACT.Identity,
                                     bias=cu[:, 0:1]).then_inc(u_ready, 1)

            d_steps(act, d_front, d_back)

            def scan_steps(first, keep):
                with act.Fori(0, LCH // 2) as i:
                    for s in (0, 1):
                        n = 2 * i + (first + s)
                        act.wait_ge(z_done, n + 1)
                        nc.scalar.activation(sg[:, s], ps[0:SD, s, 0:NCH], ACT.Silu).then_inc(silu_done, 1)
                        if keep:
                            act.wait_ge(st_ready, n + 3)
                            nc.scalar.activation(s_steps[:, 2 * i + s, :], st[:, 1 - s], ACT.Copy)\
                                .then_inc(saved, 1)

            scan_steps(0, False)
            scan_steps(LCH, True)
            act.wait_ge(saved, LCH)
            act.wait_ge(flag_ready, 1)
            good = act.value_load(flag[0:1, 0:1], min_val=0, max_val=1)
            with act.If(good == 0):
                with act.Fori(0, T // 2) as i:
                    for s in (0, 1):
                        n = 2 * i + s
                        act.wait_ge(seq_z, n + 1)
                        nc.scalar.activation(sg[:, s, 0:1], ps[0:SD, s, 0:1], ACT.Silu).then_inc(seq_silu, 1)
                        act.wait_ge(seq_st, n + 2)
                        nc.scalar.activation(s_all[0:SD, bass.ds(n, 1)], st[:, 1 - s, 0:1], ACT.Copy)\
                            .then_inc(seq_saved, 1)
                act.wait_ge(seq_saved, T)

            def f_stage(d, slot):
                wait(act, f_done, GT * (d - 1))
                nc.scalar.activation(stage[:, slot], s_all[:, bass.ds(d * GW, GW)], ACT.Copy)\
                    .then_inc(staged, 1)

            for s in (0, 1):
                f_stage(s, s)
            with act.Fori(1, X_G // 2) as i:
                for s in (0, 1):
                    f_stage(2 * i + s, s)

        @block.vector
        def _(dve):
            def layernorm(n, src, dst_free, done):
                step = [LN_STEPS * n, 0]

                def link(ins):
                    step[1] += 1
                    ins.then_inc(ln_step, 1)
                    wait_apart(dve, ln_step, step[0] + step[1], tick)

                for t in range(GT):
                    ins = nc.vector.bn_stats(stats[:, t, :], src(t))
                link(ins)
                for t in range(GT):
                    ins = nc.vector.bn_aggr(mv[:, t, :], stats[:, t, :])
                link(ins)
                link(nc.vector.tensor_scalar(ve[:, :], mv[:, :, 1], EPS, None, ALU.add))
                link(nc.vector.tensor_scalar(yi[:, :], ve[:, :].bitcast(I32), 1, None,
                                             ALU.logical_shift_right))
                link(nc.vector.tensor_scalar(ya[:, :].bitcast(I32), yi[:, :], -1, 0x5F3759DF,
                                             ALU.mult, ALU.add))
                for _ in range(3):
                    link(nc.vector.tensor_tensor(yb[:, :], ya[:, :], ya[:, :], ALU.mult))
                    link(nc.vector.scalar_tensor_tensor(out=yb[:, :], in0=yb[:, :], scalar=-0.5,
                                                        in1=ve[:, :], op0=ALU.mult, op1=ALU.mult))
                    link(nc.vector.scalar_tensor_tensor(out=ya[:, :], in0=yb[:, :], scalar=1.5,
                                                        in1=ya[:, :], op0=ALU.add, op1=ALU.mult))
                assert step[1] == LN_STEPS
                dst_free()
                for t in range(GT):
                    ins = nc.vector.tensor_scalar(xn[:, t, :], src(t), mv[:, t, 0:1], ya[:, t:t + 1],
                                                  ALU.subtract, ALU.mult)
                ins.then_inc(done, 1)

            dve.wait_ge(setup_mm, 3)
            nc.vector.tensor_copy(w_u[:, :, :].rearrange("p c s -> p (c s)"), ps[:, 0, 0:FC * SD])\
                .then_inc(setup_ev, 1)
            nc.vector.tensor_copy(cu[:, :], ps[0:SD, 1, 0:1]).then_inc(setup_ev, 1)
            nc.vector.tensor_scalar(mean[:, :], ps[0:SD, 2, 0:1], 1.0 / KEYS, None, ALU.mult)\
                .then_inc(setup_ev, 1)
            dve.wait_ge(setup_mm, 4)
            nc.vector.tensor_tensor(c_aug[SD:SD + 1, :], ps[0:1, 3, :], bp[0:1, :], ALU.add)\
                .then_inc(setup_ev, 1)

            def b_front(g, slot):
                wait_apart(dve, xs_loaded, 16 * (g + 1), tick)
                layernorm(g, lambda t: xs[:, t, :], lambda: wait(dve, transposed, 2 * g), normed)

            def b_back(g, slot, *block_half):
                if isinstance(g, int) and g >= CTX_G or block_half:
                    return
                for t in range(GT):
                    dve.wait_ge(v_done, GT * g + (t + 1))
                    nc.vector.tensor_tensor(v[:, GT * g + t, :], ps[:, 6 + t, :], bv[:, :], ALU.add)\
                        .then_inc(v_evac, 1)

            b_steps(dve, b_front, b_back)

            def own(hh):
                return slice(HD * hh, HD * hh + HD), slice(HD * (1 - hh), HD * (1 - hh) + HD)

            def k_high(hh, pr):
                a, _ = own(hh)
                nc.vector.tensor_copy(k_split[a, hh, :], kt4[a, pr, 0:KEYS]).then_inc(k_hi, 1)

            def k_low(hh, pr, part):
                a, b = own(hh)
                c = slice(0, LO_SPLIT) if part == 0 else slice(LO_SPLIT, KEYS)
                return nc.vector.tensor_tensor(k_split[b, hh, c], kt4[a, pr, c],
                                               k_split[a, hh, c].bitcast(F32), ALU.subtract)

            def q_both(hh, n):
                a, b = own(hh)
                nc.vector.tensor_copy(q_split[a, hh, 0, :], qt_sb[a, :]).then_inc(q_hi, 1)
                nc.vector.tensor_copy(q_split[b, hh, 0, :], qt_sb[a, :])
                dve.wait_ge(q_hi, n + 1)
                qh = q_split[a, hh, 0, :].bitcast(F32)
                nc.vector.tensor_tensor(q_split[a, hh, 1, :], qt_sb[a, :], qh, ALU.subtract)
                return nc.vector.tensor_tensor(q_split[b, hh, 1, :], qt_sb[a, :], qh, ALU.subtract)

            def row_chunk(u, slot, s4, c, turned_before):
                a, n = CHUNKS[c]
                dve.wait_ge(scored, NC * u + (c + 1))
                wait_apart(dve, turned, turned_before, tick)
                src = ps[:, 2 * (c % 2):2 * (c % 2) + 2, :].rearrange("p a b -> p (a b)")[:, 0:n]
                nc.vector.tensor_tensor_reduce(prow[:, slot, a:a + n], src, ones[:, 0:1].to_broadcast([P, n]),
                                               SCALE, -3.0e38, ALU.mult, ALU.max, mx[:, s4, c:c + 1])\
                    .then_inc(max_part, 1)

            def row_max(u, s4):
                wait_apart(dve, max_part, NC * (u + 1), tick)
                nc.vector.tensor_tensor_reduce(mxn[:, s4, :], mx[:, s4, :], zeros[:, :], -1.0, 3.0e38,
                                               ALU.add, ALU.min, negm[:, s4:s4 + 1]).then_inc(neg_max, 1)

            def reciprocal_sum(u, s4):
                dve.wait_ge(exped, 2 * (u + 1))
                nc.vector.tensor_tensor(dsum[:, s4:s4 + 1], den[:, s4, 0:1], den[:, s4, 1:2], ALU.add)\
                    .then_inc(den_sum, 1)
                dve.wait_ge(den_sum, u + 1)
                nc.vector.reciprocal(rden[:, s4:s4 + 1], dsum[:, s4:s4 + 1]).then_inc(rden_ready, 1)

            def take_half(u, slot):
                dve.wait_ge(pv_done, NGR * (u + 1))
                wait(dve, folded, u - 1)
                nc.vector.tensor_copy(o_half[:, slot, :], ps[:, 6 + slot, 0:P]).then_inc(half_ready, 1)

            def scale_out(it, u, j):
                hh, q = j // QT_N, j % QT_N
                dve.wait_ge(folded, u + 1)
                dve.wait_ge(rden_ready, u + 1)
                if q == 0:
                    wait(dve, (o_even_stored, o_odd_stored)[hh], 16 * it)
                nc.vector.tensor_scalar(o_out[:, hh, q, :], ps[:, 6 + j % 2, P:P + HD],
                                        rden[:, j % 4:j % 4 + 1], None, ALU.mult).then_inc(o_scaled, 1)

            dve.wait_ge(p_padded, 1)
            dve.wait_ge(kq_evac, FC * NG)
            dve.wait_ge(qt_loaded, 16)
            k_high(0, 0)
            dve.wait_ge(k_hi, 1)
            for part in (0, 1):
                k_low(0, 0, part)
            q_both(0, 0).then_inc(even_ready, 1)
            for u in (0, 1):
                for c in range(NC):
                    row_chunk(u, u, u, c, 0)
                row_max(u, u)
            k_high(1, 0)

            def c_body(it, first=False, last=False):
                for j in range(UNITS):
                    u = UNITS * it + j
                    reciprocal_sum(u, j % 4)
                    if not (first and j == 0):
                        take_half(u - 1, (j + 1) % 2)
                    for c in range(NC):
                        if not (last and j >= UNITS - 2):
                            row_chunk(u + 2, j % 2, (j + 2) % 4, c, NGR * u + min(2 * c + 2, NGR))
                        if c == 1 and not (first and j == 0):
                            scale_out(it if j else it - 1, u - 1, (j + UNITS - 1) % UNITS)
                    if not (last and j >= UNITS - 2):
                        row_max(u + 2, (j + 2) % 4)
                    nxt = 0 if last else (it + 1) % PAIRS
                    if j == 0:
                        q_both(1, 2 * it + 1).then_inc(qt_used, 1)
                        dve.wait_ge(k_hi, 2 * it + 2)
                        k_low(1, it % PAIRS, 0)
                    if j == 1:
                        k_low(1, it % PAIRS, 1).then_inc(odd_ready, 1)
                    if last:
                        continue
                    if j == 2:
                        k_high(0, nxt)
                    if j == 3:
                        dve.wait_ge(k_hi, 2 * it + 3)
                        k_low(0, nxt, 0)
                    if j == 4:
                        k_low(0, nxt, 1)
                    if j == 5:
                        dve.wait_ge(qt_loaded, 16 * (it + 2))
                        q_both(0, 2 * it + 2).then_inc(even_ready, 1)
                    if j == 7:
                        k_high(1, nxt)

            c_steps(dve, c_body)
            take_half(UNITS * ITERS - 1, 1)
            scale_out(ITERS - 1, UNITS * ITERS - 1, UNITS - 1)

            def d_front(d, slot):
                dve.wait_ge(xb_ready, d + 1)
                for t in range(GT):
                    dve.wait_ge(y_done, GT * d + (t + 1))
                    nc.vector.tensor_tensor(x1[:, GT * d + t, :], ps[:, 2 + t, :], xb[:, slot, t], ALU.add)\
                        .then_inc(x1_ready, 1)
                wait_apart(dve, x1_ready, GT * (d + 1), tick)
                layernorm(d + NG, lambda t: x1[:, GT * d + t, :], lambda: wait(dve, n2_turned, 2 * d),
                          normed2)

            d_steps(dve, d_front, lambda d, slot: None)

            dve.wait_ge(u_ready, X_G)
            nc.vector.memset(s_all[SD:SD + 1, :], 1.0)
            nc.vector.memset(st[:, 0], 0.0).then_inc(st_ready, 1)

            def scan_steps(first):
                with dve.Fori(0, LCH // 2) as i:
                    for s in (0, 1):
                        n = 2 * i + (first + s)
                        dve.wait_ge(silu_done, n + 1)
                        if first:
                            wait(dve, saved, 2 * i + s) if s else None
                        nc.vector.tensor_tensor(st[:, 1 - s], sg[:, s], u_steps[:, 2 * i + s, :], ALU.add)\
                            .then_inc(st_ready, 1)

            scan_steps(0)
            dve.wait_ge(st_ready, LCH + 1)
            nc.vector.tensor_copy(end1, st[:, 0]).then_inc(cmp_step, 1)
            dve.wait_ge(cmp_step, 1)
            nc.vector.memset(st[:, 0, 0:1], 0.0)
            nc.vector.tensor_copy(st[:, 0, 1:NCH], end1[:, 0:NCH - 1]).then_inc(st_ready, 1)
            scan_steps(LCH)
            dve.wait_ge(st_ready, 2 * LCH + 2)
            nc.vector.tensor_tensor(diff, st[:, 0], end1, ALU.subtract).then_inc(cmp_step, 1)
            dve.wait_ge(cmp_step, 2)
            nc.vector.tensor_tensor(sq[:, 0], diff, diff, ALU.mult)
            nc.vector.tensor_tensor(sq[:, 1], st[:, 0], st[:, 0], ALU.mult).then_inc(cmp_step, 1)
            dve.wait_ge(sums_done, 1)
            nc.vector.tensor_copy(e_row, ps[0:1, 3, 0:NCH]).then_inc(cmp_step, 1)
            dve.wait_ge(cmp_step, 4)
            nc.vector.scalar_tensor_tensor(out=lhs_row, in0=e_row, scalar=-TOL2, in1=ps[0:1, 2, 0:NCH],
                                           op0=ALU.mult, op1=ALU.add).then_inc(cmp_step, 1)
            dve.wait_ge(cmp_step, 5)
            nc.vector.tensor_scalar(ok_row, lhs_row, 0.0, None, ALU.is_le).then_inc(cmp_step, 1)
            dve.wait_ge(cmp_step, 6)
            nc.vector.tensor_reduce(flag_f[:, 0:1], ok_row, AX_X, ALU.min).then_inc(cmp_step, 1)
            dve.wait_ge(cmp_step, 7)
            nc.vector.tensor_copy(flag[:, :], flag_f[:, 0:1]).then_inc(flag_ready, 1)
            dve.wait_ge(flag_ready, 1)
            good = dve.value_load(flag[0:1, 0:1], min_val=0, max_val=1)
            with dve.If(good == 0):
                dve.wait_ge(saved, LCH)
                nc.vector.memset(st[:, 0, 0:1], 0.0).then_inc(seq_st, 1)
                with dve.Fori(0, T // 2) as i:
                    for s in (0, 1):
                        n = 2 * i + s
                        dve.wait_ge(seq_silu, n + 1)
                        nc.vector.tensor_tensor(st[:, 1 - s, 0:1], sg[:, s, 0:1], u_all[:, bass.ds(n, 1)],
                                                ALU.add).then_inc(seq_st, 1)

            def f_add(d, slot):
                for t in range(GT):
                    dve.wait_ge(f_done, GT * d + (t + 1))
                    nc.vector.tensor_tensor(x1[:, GT * d + t, :], ps[:, 4 + 2 * slot + t, :],
                                            x1[:, GT * d + t, :], ALU.add).then_inc(f_added, 1)

            with dve.Fori(0, X_G // 2) as i:
                for s in (0, 1):
                    f_add(2 * i + s, s)

        @block.tensor
        def _(pe):
            mm = nc.tensor.matmul
            pe.wait_ge(setup_loaded, 16 * 10)
            pe.wait_ge(consts, 7)
            for m in range(FC):
                for k in range(FC):
                    ins = mm(ps[:, 0, m * SD:(m + 1) * SD], win_sb[:, k, m * P:(m + 1) * P], b_sb[:, k, :],
                             start=(k == 0), stop=(k == FC - 1))
            ins.then_inc(setup_mm, 1)
            for k in range(FC):
                ins = mm(ps[0:SD, 1, 0:1], b_sb[:, k, :], bin_[:, k:k + 1], start=(k == 0), stop=(k == FC - 1))
            ins.then_inc(setup_mm, 1)
            for t in range(KT_TILES):
                ins = mm(ps[0:SD, 2, 0:1], cb_sb[:, t, :], ones[:, :], start=(t == 0), stop=(t == KT_TILES - 1))
            ins.then_inc(setup_mm, 1)
            pe.wait_ge(setup_ev, 3)
            mm(ps[0:1, 3, :], mean[:, :], wp_sb, start=True, stop=True).then_inc(setup_mm, 1)
            pe.wait_ge(setup_ev, 4)

            def b_front(g, slot):
                pe.wait_ge(normed, g + 1)
                wait(pe, nt_ready, FC * g)
                for c in range(FC):
                    for t in range(GT):
                        ins = nc.tensor.transpose(ps[:, c // 2, (c % 2) * GW + t * P:(c % 2) * GW + (t + 1) * P],
                                                  xn[:, t, c * P:(c + 1) * P], ident[:, :])
                    if c % 2:
                        ins.then_inc(transposed, 1)

            def b_back(g, slot, *block_half):
                is_ctx = isinstance(g, int) and g < CTX_G or not isinstance(g, int) and not block_half
                pe.wait_ge(nt_ready, FC * (g + 1))
                if isinstance(g, int) and g == 0:
                    pe.wait_ge(w_loaded, 16)
                if is_ctx:
                    for t in range(GT):
                        wait(pe, v_evac, GT * (g - 1) + (t + 1))
                        for k in range(FC):
                            ins = mm(ps[:, 6 + t, :], nt[:, slot, k, t * P:(t + 1) * P], w3[:, 2, k, :],
                                     start=(k == 0), stop=(k == FC - 1))
                        ins.then_inc(v_done, 1)
                for c in range(FC):
                    wait(pe, kq_evac, FC * (g - 1) + (c + 1))
                    for k in range(FC):
                        ins = mm(ps[:, 2 + c, 0:GW], w3[:, 1 if is_ctx else 0, k, c * P:(c + 1) * P],
                                 nt[:, slot, k, :], start=(k == 0), stop=(k == FC - 1))
                    ins.then_inc(kq_done, 1)

            b_steps(pe, b_front, b_back)

            def scores(u, hh, q, c):
                a, n = CHUNKS[c]
                wait(pe, max_part, NC * u + (c - 1))
                for o in range(0, n, 512):
                    w = min(512, n - o)
                    for part in (0, 1):
                        ins = mm(ps[:, 2 * (c % 2) + o // 512, 0:w], q_split[:, hh, part, q * P:(q + 1) * P],
                                 k_split[:, hh, a + o:a + o + w], start=(part == 0), stop=(part == 1))
                ins.then_inc(scored, 1)

            def turn(u, j, g):
                G = NGR * u + g
                pe.wait_ge(exped, 2 * u + (2 if GROUPS[g][-1] * P >= EXP_SPLIT else 1))
                wait(pe, pt_ready, G - 1)
                for i, t in enumerate(GROUPS[g]):
                    ins = nc.tensor.transpose(ps[:, 4 + (NGR * j + g) % 2, i * P:(i + 1) * P],
                                              prow[:, j % 2, t * P:(t + 1) * P], ident[:, :])
                ins.then_inc(turned, 1)

            def pv(u, j, g):
                if g == 0:
                    wait(pe, o_scaled, u - 1)
                pe.wait_ge(pt_ready, NGR * u + (g + 1))
                for i, t in enumerate(GROUPS[g]):
                    r = HD * (t % 2)
                    ins = mm(ps[r:r + HD, 6 + j % 2, 0:P], v_head[:, j // QT_N, t, :],
                             pt_sb[:, (NGR * j + g) % 2, i * P:(i + 1) * P],
                             start=(t < 2), stop=(t >= KT_TILES - 2))
                ins.then_inc(pv_done, 1)

            def fold_out(u, slot):
                pe.wait_ge(half_ready, u + 1)
                mm(ps[:, 6 + slot, P:P + HD], o_half[:, slot, :], fold[:, :], start=True, stop=True)\
                    .then_inc(folded, 1)

            pe.wait_ge(kq_evac, FC * NG)
            pe.wait_ge(v_evac, GT * CTX_G)
            pe.wait_ge(even_ready, 1)
            for u in (0, 1):
                for c in range(NC):
                    scores(u, 0, u, c)

            def c_body(it, first=False, last=False):
                for j in range(UNITS):
                    u = UNITS * it + j
                    j2 = (j + 2) % UNITS
                    more = not (last and j >= UNITS - 2)

                    def next_scores(c):
                        if more:
                            scores(u + 2, j2 // QT_N, j2 % QT_N, c)

                    if j == 0:
                        pe.wait_ge(vh_even, it + 1)
                    if j == QT_N:
                        pe.wait_ge(vh_odd, it + 1)
                    turn(u, j, 0)
                    turn(u, j, 1)
                    if j2 == QT_N:
                        pe.wait_ge(odd_ready, it + 1)
                    if j2 == 0 and more:
                        pe.wait_ge(even_ready, it + 2)
                    next_scores(0)
                    pv(u, j, 0)
                    turn(u, j, 2)
                    if not (first and j == 0):
                        fold_out(u - 1, (j + 1) % 2)
                    pv(u, j, 1)
                    turn(u, j, 3)
                    next_scores(1)
                    pv(u, j, 2)
                    turn(u, j, 4)
                    pv(u, j, 3)
                    turn(u, j, 5)
                    next_scores(2)
                    pv(u, j, 4)
                    turn(u, j, 6)
                    pv(u, j, 5)
                    next_scores(3)
                    pv(u, j, 6)

            c_steps(pe, c_body)
            fold_out(UNITS * ITERS - 1, 1)

            def d_front(d, slot):
                pe.wait_ge(og_loaded, 16 * GT * (d + 1))
                wait(pe, ot_ready, 2 * d)
                for c in range(FC):
                    for t in range(GT):
                        ins = nc.tensor.transpose(ps[:, c // 2, (c % 2) * GW + t * P:(c % 2) * GW + (t + 1) * P],
                                                  work[:, t * H + c * P:t * H + (c + 1) * P], ident[:, :])
                    if c % 2:
                        ins.then_inc(o_turned, 1)
                pe.wait_ge(ot_ready, 2 * (d + 1))
                for t in range(GT):
                    wait(pe, x1_ready, GT * (d - 1) + (t + 1))
                    for k in range(FC):
                        ins = mm(ps[:, 2 + t, :], ot[:, slot, k, t * P:(t + 1) * P], wo_qo[:, k, :],
                                 start=(k == 0), stop=(k == FC - 1))
                    ins.then_inc(y_done, 1)

            def d_back(d, slot):
                pe.wait_ge(normed2, d + 1)
                wait(pe, n2t_ready, FC * d)
                for c in range(FC):
                    for t in range(GT):
                        ins = nc.tensor.transpose(
                            ps[:, 4 + c // 2, (c % 2) * GW + t * P:(c % 2) * GW + (t + 1) * P],
                            xn[:, t, c * P:(c + 1) * P], ident[:, :])
                    if c % 2:
                        ins.then_inc(n2_turned, 1)
                pe.wait_ge(n2t_ready, FC * (d + 1))
                wait(pe, u_ready, d)
                for k in range(FC):
                    ins = mm(ps[0:SD, 6, 0:GW], w_u[:, k, :], nt[:, slot, k, :],
                             start=(k == 0), stop=(k == FC - 1))
                ins.then_inc(u_done, 1)

            pe.wait_ge(wo_loaded, 16)
            pe.wait_ge(o_scaled, UNITS * ITERS)
            d_steps(pe, d_front, d_back)

            def scan_steps(first):
                with pe.Fori(0, LCH // 2) as i:
                    for s in (0, 1):
                        n = 2 * i + (first + s)
                        wait_apart(pe, st_ready, n + (2 if first else 1), tick)
                        mm(ps[0:SD, s, 0:NCH], at[:, :], st[:, s], start=True, stop=True).then_inc(z_done, 1)

            scan_steps(0)
            scan_steps(LCH)
            pe.wait_ge(cmp_step, 3)
            for k in (0, 1):
                ins = mm(ps[0:1, 2 + k, 0:NCH], ones[0:SD, :], sq[:, k], start=True, stop=True)
            ins.then_inc(sums_done, 1)
            pe.wait_ge(flag_ready, 1)
            good = pe.value_load(flag[0:1, 0:1], min_val=0, max_val=1)
            with pe.If(good == 0):
                with pe.Fori(0, T // 2) as i:
                    for s in (0, 1):
                        wait_apart(pe, seq_st, 2 * i + (s + 1), tick)
                        mm(ps[0:SD, s, 0:1], at[:, :], st[:, s, 0:1], start=True, stop=True).then_inc(seq_z, 1)

            def f_mm(d, slot):
                pe.wait_ge(staged, d + 1)
                for t in range(GT):
                    wait(pe, f_added, GT * (d - 2) + (t + 1))
                    mm(ps[:, 4 + 2 * slot + t, :], stage[:, slot, t * P:(t + 1) * P], c_aug[:, :],
                       start=True, stop=True).then_inc(f_done, 1)

            for s in (0, 1):
                f_mm(s, s)
            with pe.Fori(1, X_G // 2) as i:
                for s in (0, 1):
                    f_mm(2 * i + s, s)


def kernel(**inputs):
    import numpy as np
    import concourse.bacc as bacc
    from concourse.bass_utils import run_bass_kernel_spmd

    g = {k.replace("L0_xattn_", ""): np.asarray(a) for k, a in inputs.items()}

    def column(a):
        return a.reshape(FC, P).T

    def padded(a):
        return np.concatenate([a, np.zeros((KPAD - KEYS, a.shape[1]), a.dtype)], axis=0)

    b_q, b_k, b_v = g["b_qkv"].reshape(3, H)
    arrays = {
        "x": g["x"].reshape(T, H),
        "ctx": padded(g["ctx_1024"].reshape(KEYS, H)),
        "ctxb": padded(g["ctxb_2048x64"].reshape(KEYS, SD)).reshape(KT_TILES, P, SD).transpose(1, 0, 2),
        "w_qkv_t": g["W_qkv"].reshape(3, H, FC, P).transpose(3, 0, 2, 1),
        "w_o_t": g["W_o"].reshape(H, FC, P).transpose(2, 1, 0),
        "w_in": g["W_in"].reshape(FC, P, H).transpose(1, 0, 2),
        "bmat": g["Bmat"].reshape(FC, P, SD).transpose(1, 0, 2),
        "w_prog_t": g["W_prog"].T,
        "a_t": g["A"].T,
        "cmat": g["Cmat"],
        "cols": np.stack([column(a) for a in (g["g1"], g["beta1"], g["g2"], g["beta2"], b_q, b_k, g["b_in"])],
                         axis=1),
        "bv_rows": np.broadcast_to(b_v, (P, H)),
        "bo_rows": np.broadcast_to(g["b_o"], (P, H)),
        "b_prog": g["b_prog"].reshape(1, H),
    }
    arrays = {k: np.ascontiguousarray(a) for k, a in arrays.items()}
    nc = bacc.Bacc("TRN2", target_bir_lowering=False, num_devices=1)
    args = [nc.dram_tensor(k, list(a.shape), mybir.dt.from_np(a.dtype), kind="ExternalInput").ap()
            for k, a in arrays.items()]
    out = nc.dram_tensor("out", [T, H], F32, kind="ExternalOutput").ap()
    build(nc, *args, out)
    r = run_bass_kernel_spmd(nc, [arrays], core_ids=[0])
    return r.results[0]["out"].reshape(1, T, H)
```

```python
from contextlib import ExitStack

import concourse.bass as bass
from concourse import mybir

F32 = mybir.dt.float32
F32R = mybir.dt.float32r
I32 = mybir.dt.int32
ALU = mybir.AluOpType
ACT = mybir.ActivationFunctionType
AX_X = mybir.AxisListType.X

P = 128
T = 4096
KEYS = 3202
KT_TILES = -(-KEYS // P)
KPAD = KT_TILES * P
H = 512
FC = H // P
NH = 8
HD = H // NH
SD = 64
EPS = 1e-5
SCALE = HD ** -0.5

GT = 2
GW = GT * P
CTX_G = KPAD // GW
X_G = T // GW
NG = CTX_G + X_G

QB = 512
QT_N = QB // P
PAIRS = NH // 2
ITERS = (T // QB) * PAIRS
NP = KT_TILES // 2
UNIT_N = 2 * ITERS
PW = 2 * P
MAX_AT = [(0,), (1,), (2,), (3, 4)] + [(s + 1,) for s in range(4, NP - 1)] + [()]
NM = 3 * QT_N + 1
TAIL = 3072
PIECES = [(0, 1024), (1024, 2048), (2048, 3072), (3072, KPAD)]
PAD_SCORE = -2.0 ** 100
PT_SLOTS = 4

LCH = 16
NCH = T // LCH
TOL2 = 2.0 ** -38

MOD_LO = 96

LN_STEPS = 14


def wait(eng, sem, value):
    if not (isinstance(value, int) and value <= 0):
        eng.wait_ge(sem, value)


def wait_apart(eng, sem, value, tick):
    wait(eng, sem, value)
    if not isinstance(value, int):
        eng.sem_inc(tick, 1)


def pt_slot(w2, s):
    return (NP * w2 + s) % PT_SLOTS


def pt_user_before(w, w2, s):
    i = NP * w2 + s
    j = i - PT_SLOTS if i >= PT_SLOTS else max(k for k in range(2 * NP) if k % PT_SLOTS == i) - 2 * NP
    return w - w2 + j // NP, j % NP


def pe_sum_index(s):
    return max(s // 2 - 1, 0)


SUMS_V = NP // 2 + 1
SUMS_G = NP // 2 + 1


def build(nc, x, ctx, ctxb, w_qkv_t, w_o_t, w_in, bmat, w_prog_t, a_t, cmat, cols, bv_rows, bo_rows,
          b_prog, k2_rows, out):
    es = ExitStack()
    with es:
        def sb(name, shape, dt=F32):
            return es.enter_context(nc.sbuf_tensor(name, shape, dt))

        def sem(name):
            return es.enter_context(nc.semaphore(name))

        q_scratch = nc.dram_tensor("q_scratch", [ITERS, P, QB], F32).ap()
        o_scratch = nc.dram_tensor("o_scratch", [ITERS, 2, P, QT_N * HD], F32).ap()

        kt = sb("kt", [P, FC * KPAD])
        big = sb("big", [P, KT_TILES * H + 3 * FC * H])
        k1 = sb("k1", [P, 2, KPAD], F32R)
        k2 = sb("k2", [P, KPAD], F32R)
        q_max = sb("q_max", [P, QB], F32R)
        q1 = sb("q1", [P, 2, QB], F32R)
        q2 = sb("q2", [HD + 2, 2, QB], F32R)
        work = sb("work", [P, 4096])
        wo_qo = sb("wo_qo", [P, FC, H])
        qt_sb = sb("qt_sb", [P, QB])[:, :]
        k2_cols = sb("k2_cols", [HD + 2, 2])
        w_u = sb("w_u", [P, FC, SD])
        ident = sb("ident", [P, P])
        fold = sb("fold", [P, HD])
        ones = sb("ones", [P, 1])
        col = sb("col", [P, 7, FC])
        c_aug = sb("c_aug", [SD + 1, H])
        cu = sb("cu", [SD, 1])
        mean = sb("mean", [SD, 1])
        stats = sb("stats", [P, GT, 6])
        mv = sb("mv", [P, GT, 2])
        ve = sb("ve", [P, GT])
        yi = sb("yi", [P, GT], I32)
        ya = sb("ya", [P, GT])
        yb = sb("yb", [P, GT])
        mx_part = sb("mx_part", [P, QT_N, 4])
        mx_first = sb("mx_first", [P, QT_N, 7])
        mx = sb("mx", [P, QT_N])
        rden = sb("rden", [P, QT_N])
        flag_f = sb("flag_f", [1, 2])
        flag = sb("flag", [1, 1], I32)
        ps = es.enter_context(nc.psum_tensor("ps", [P, 8, 512], F32))

        g1, be1, g2, be2, bq, bk, bin_ = (col[:, i, :] for i in range(7))
        kt4 = kt[:, :].rearrange("p (c k) -> p c k", c=FC)
        v = big[:, 0:KT_TILES * H].rearrange("p (t f) -> p t f", t=KT_TILES)
        pt = big[:, KT_TILES * H:KT_TILES * H + PT_SLOTS * 2 * QB].rearrange("p (s k) -> p s k", s=PT_SLOTS)
        sums = big[:, KT_TILES * H + PT_SLOTS * 2 * QB:].rearrange("p (e k) -> p e k", e=2)
        bv = wo_qo[:, 3, :]
        at = wo_qo[0:SD, 3, 0:2 * SD]
        qt_first = wo_qo[:, 0, :]
        o_half = wo_qo[:, 1, :]
        o_out = wo_qo[:, 2, :].rearrange("p (h q d) -> p h q d", h=2, q=QT_N)
        w3 = big[:, KT_TILES * H:KT_TILES * H + 3 * FC * H].rearrange("p (w c n) -> p w c n", w=3, c=FC)
        win_sb = v[:, 22:26, :]
        b_sb = v[:, 21, 0:FC * SD].rearrange("p (c s) -> p c s", c=FC)
        cb_sb = big[:, 17 * H:17 * H + KT_TILES * SD].rearrange("p (t s) -> p t s", t=KT_TILES)
        wp_sb = v[0:SD, 16, :]
        bp = v[0:1, 15, :]
        xs = work[:, 0:2048].rearrange("p (s t f) -> p s t f", s=2, t=GT)
        xn = work[:, 1024:2048].rearrange("p (t f) -> p t f", t=GT)
        nt = work[:, 2048:4096].rearrange("p (s c k) -> p s c k", s=2, c=FC)
        v_head = work[:, 0:2 * KT_TILES * HD].rearrange("p (s t d) -> p s t d", s=2, t=KT_TILES)
        s_all = kt[0:SD, 0:T + 1]
        u_all = kt[SD:2 * SD, 0:T]
        a = T + 4
        og = kt[:, a:a + 2048].rearrange("p (s t h d) -> p s t h d", s=2, t=GT, h=NH)
        w_o = kt[:, a + 2048:a + 4096].rearrange("p (c n) -> p c n", c=FC)
        ot = kt[:, a + 4096:a + 6144].rearrange("p (s c k) -> p s c k", s=2, c=FC)
        xb = kt[:, a + 6144:a + 8192].rearrange("p (s t f) -> p s t f", s=2, t=GT)
        bo = kt[:, a + 8192:a + 8192 + H]
        x1 = big[:, 0:(T // P) * H].rearrange("p (t f) -> p t f", t=T // P)
        st = work[0:SD, 0:2 * NCH].rearrange("p (s c) -> p s c", s=2)
        sg = work[SD:2 * SD, 0:NCH]
        end1 = work[0:SD, 1024:1024 + NCH]
        diff = work[0:SD, 1280:1280 + NCH]
        sq = work[0:SD, 1536:1536 + 2 * NCH].rearrange("p (s c) -> p s c", s=2)
        lhs_row = work[0:1, 2048:2048 + NCH]
        ok_row = work[0:1, 2304:2304 + NCH]
        e_row = work[0:1, 2560:2560 + NCH]
        u_steps = u_all.rearrange("p (c k) -> p k c", k=LCH)
        s_from = s_all[:, 0:T].rearrange("p (c k) -> p k c", k=LCH)
        s_to = s_all[:, 1:T + 1].rearrange("p (c k) -> p k c", k=LCH)
        c1 = k1[:, 0, 0:H]
        c2 = k2[0:MOD_LO + 1, 0:H]
        s1 = k1[:, 1, 0:2 * GW].rearrange("p (s k) -> p s k", s=2)
        s2 = k2[0:MOD_LO + 1, H:H + 2 * GW].rearrange("p (s k) -> p s k", s=2)

        setup_loaded = sem("setup_loaded"); w_loaded = sem("w_loaded"); wo_loaded = sem("wo_loaded")
        consts = sem("consts"); setup_mm = sem("setup_mm"); setup_ev = sem("setup_ev")
        ln_step = sem("ln_step")
        tick = sem("tick")
        xs_loaded = [sem("xs_loaded_0"), sem("xs_loaded_1")]; normed = sem("normed"); transposed = sem("transposed")
        nt_ready = sem("nt_ready"); kq_done = sem("kq_done"); kq_evac = sem("kq_evac")
        v_done = sem("v_done"); v_evac = sem("v_evac"); q_stored = [sem("q_stored_0"), sem("q_stored_1")]
        qt_loaded = sem("qt_loaded"); bo_loaded = sem("bo_loaded"); at_loaded = sem("at_loaded")
        q2_ones_set = sem("q2_ones_set"); k2_rows_set = sem("k2_rows_set")
        k_hi = sem("k_hi"); k_lo = sem("k_lo"); k2_ready = sem("k2_ready")
        qm_ready = sem("qm_ready"); q1_ready = sem("q1_ready"); q2_ready = sem("q2_ready")
        v_even_loaded = sem("v_even_loaded"); v_odd_loaded = sem("v_odd_loaded")
        max_done = sem("max_done"); max_taken = sem("max_taken"); first_free = sem("first_free"); max_ready = sem("max_ready")
        max_turned = sem("max_turned"); shift_ready = sem("shift_ready")
        scored = sem("scored"); exped = sem("exped"); pv_done = sem("pv_done")
        summed_v = sem("summed_v"); summed_g = sem("summed_g"); half_ready = sem("half_ready")
        folded = sem("folded"); rden_ready = sem("rden_ready"); o_scaled = sem("o_scaled")
        o_even_free = sem("o_even_free"); o_odd_free = sem("o_odd_free")
        og_loaded = [sem("og_loaded_0"), sem("og_loaded_1")]; x2_loaded = [sem("x2_loaded_0"), sem("x2_loaded_1")]; xb_ready = sem("xb_ready")
        o_turned = sem("o_turned"); ot_ready = sem("ot_ready"); y_done = sem("y_done")
        x1_ready = sem("x1_ready"); normed2 = sem("normed2"); n2_turned = sem("n2_turned")
        n2t_ready = sem("n2t_ready"); u_done = sem("u_done"); u_ready = sem("u_ready")
        z_done = sem("z_done"); silu_done = sem("silu_done"); st_ready = sem("st_ready")
        cmp_step = sem("cmp_step"); sums_done = sem("sums_done")
        flag_ready = sem("flag_ready")
        seq_z = sem("seq_z"); seq_silu = sem("seq_silu"); seq_st = sem("seq_st")
        c_cleared = sem("c_cleared"); c_hi = sem("c_hi"); c_ready = sem("c_ready"); s_hi = sem("s_hi"); s_lo = sem("s_lo"); f_done = sem("f_done"); f_added = sem("f_added"); stored = sem("stored")

        block = es.enter_context(nc.Block())

        def b_steps(eng, front, back, after=lambda g: None,
                    before=lambda i, s: None, inside=lambda i, s: None):
            front(0, 0, 1)
            for g in (0, 1):
                front(g + 1, (g + 1) % 2, (g + 1) // 2 + 1)
                back(g, g % 2)
            with eng.Fori(0, 5) as i:
                for s in (0, 1):
                    front(2 * i + (3 + s), (1 + s) % 2, i + (2 + s))
                    back(2 * i + (2 + s), s)
            for g in (12, 13, 14):
                front(g + 1, (g + 1) % 2, (g + 1) // 2 + 1)
                back(g, g % 2)
                after(g)
            with eng.Fori(0, 6) as i:
                for s in (0, 1):
                    before(i, s)
                    front(2 * i + (16 + s), s, i + 9)
                    inside(i, s)
                    back(2 * i + (15 + s), 1 - s, i + 1, s)
            front(NG - 1, (NG - 1) % 2, (NG - 1) // 2 + 1)
            back(NG - 2, (NG - 2) % 2)
            after(NG - 2)
            back(NG - 1, (NG - 1) % 2)
            after(NG - 1)

        def x_group(g, block_half):
            return block_half or ((g - CTX_G) // 2, (g - CTX_G) % 2)

        def d_steps(eng, turn, project, turn2, finish):
            def step(d, slot, more=True, first=False):
                project(d + 1, 1 - slot, 0)
                if not first:
                    finish(d - 1, 1 - slot)
                project(d + 1, 1 - slot, 1)
                if more:
                    turn(d + 2, slot)
                turn2(d, slot)

            turn(0, 0)
            turn(1, 1)
            for t in range(GT):
                project(0, 0, t)
            for d in (0, 1):
                step(d, d, first=(d == 0))
            with eng.Fori(0, 6) as i:
                for s in (0, 1):
                    step(2 * i + (2 + s), s)
            step(X_G - 2, 0, False)
            turn2(X_G - 1, 1)
            finish(X_G - 2, 0)
            finish(X_G - 1, 1)

        def scan_halves():
            return ((h, slice(h * NCH // 2, (h + 1) * NCH // 2)) for h in (0, 1))

        def c_steps(eng, unit):
            for hh in (0, 1):
                unit(0, hh, True, False)
            with eng.Fori(1, ITERS - 1) as it:
                for hh in (0, 1):
                    unit(it, hh, False, False)
            for hh in (0, 1):
                unit(ITERS - 1, hh, False, True)

        def ahead(it, hh, n):
            k = hh + n
            return 2 * it + k, it + k // 2, k % 2

        @block.sync
        def _(sp):
            for dst, src in ((b_sb, bmat), (win_sb, w_in), (cb_sb, ctxb), (wp_sb, w_prog_t),
                             (col[:, :, :], cols), (bp, b_prog),
                             (c_aug[0:SD, :], cmat), (bv, bv_rows),
                             (k2_cols[HD:HD + 2, :], k2_rows)):
                sp.dma_start(dst, src).then_inc(setup_loaded, 16)

            def load_ctx(g, slot):
                wait(sp, transposed, 2 * (g - 1))
                sp.dma_start(xs[:, slot], ctx.rearrange("(g t p) f -> g p t f", p=P, t=GT)[g])\
                    .then_inc(xs_loaded[slot], 16)

            def load_x(h, slot):
                wait(sp, transposed, 2 * (h + CTX_G - 1))
                sp.dma_start(xs[:, slot], x.rearrange("(g t p) f -> g p t f", p=P, t=GT)[h])\
                    .then_inc(xs_loaded[slot], 16)

            def store_q(h, blk, half):
                wait(sp, kq_evac, FC * (h + CTX_G + 1))
                dst = q_scratch.rearrange("(b c) p k -> b p c k", c=FC)[blk]
                sp.dma_start(dst[:, :, half * GW:(half + 1) * GW],
                             wo_qo[:, :, half * GW:(half + 1) * GW]).then_inc(q_stored[half], 16)

            def v_copy(w, it, hh):
                wait(sp, pv_done, NP * (w - 1))
                vv = v.rearrange("p t (c s d) -> p c s t d", c=FC, s=2)
                sp.dma_start(v_head[:, hh], vv[:, it % PAIRS, hh]).then_inc((v_even_loaded, v_odd_loaded)[hh], 16)

            load_ctx(0, 0)
            sp.dma_start(w3, w_qkv_t).then_inc(w_loaded, 16)
            load_ctx(1, 1)
            with sp.Fori(1, CTX_G // 2) as i:
                for s in (0, 1):
                    load_ctx(2 * i + s, s)
            load_ctx(CTX_G - 1, 0)
            for h in (0, 1, 2):
                load_x(h, (CTX_G + h) % 2)
            for s in (0, 1):
                load_x(3 + s, s)
                store_q(s, 0, s)
            for half in (0, 1):
                sp.wait_ge(q_stored[half], 16)
            sp.dma_start(qt_sb, q_scratch[0]).then_inc(qt_loaded, 16)
            with sp.Fori(1, X_G // 2 - 2) as i:
                for s in (0, 1):
                    load_x(2 * i + (3 + s), s)
                    store_q(2 * i + s, i, s)
            load_x(X_G - 1, 0)
            for h in range(X_G - 4, X_G - 1):
                store_q(h, h // 2, h % 2)
            sp.wait_ge(transposed, 2 * NG)
            v_copy(0, 0, 0)
            store_q(X_G - 1, X_G // 2 - 1, 1)
            for half in (0, 1):
                sp.wait_ge(q_stored[half], 16 * (X_G // 2))
            for half in (0, 1):
                sp.dma_start(at[:, half * SD:(half + 1) * SD], a_t).then_inc(at_loaded, 16)

            def store_o(it, hh):
                dst = o_scratch[it, hh]
                sp.wait_ge(o_scaled, 2 * it + hh + 1)
                sp.dma_start(dst, o_out[:, hh, :, :].rearrange("p q d -> p (q d)"))\
                    .then_inc((o_even_free, o_odd_free)[hh], 16)

            def c_unit(it, hh, first, last):
                if not (last and hh == 1):
                    v_copy(*ahead(it, hh, 1))
                if hh == 0:
                    if not first:
                        store_o(it - 1, 1)
                    if not last:
                        sp.wait_ge(q2_ready, 2 * it + 2)
                        sp.dma_start(qt_sb, q_scratch[it + 1]).then_inc(qt_loaded, 16)
                else:
                    store_o(it, 0)

            def load_og(half, blk):
                src = o_scratch.rearrange("(b c) h p k -> b p (c h) k", c=FC)[blk]
                for t in range(GT):
                    q = half * GT + t
                    sp.dma_start(og[:, half, t], src[:, :, q * HD:(q + 1) * HD]).then_inc(og_loaded[half], 16)

            def load_x2(d, half):
                sp.dma_start(xb[:, half], x.rearrange("(g t p) f -> g p t f", p=P, t=GT)[d])\
                    .then_inc(x2_loaded[half], 16)

            c_steps(sp, c_unit)
            sp.wait_ge(k_lo, 4 * UNIT_N)
            sp.wait_ge(k2_ready, 4 * UNIT_N)
            sp.dma_start(w_o, w_o_t).then_inc(wo_loaded, 16)
            sp.dma_start(bo, bo_rows).then_inc(bo_loaded, 16)
            sp.wait_ge(o_odd_free, 16 * ITERS)
            for half in (0, 1):
                load_og(half, 0)
                load_x2(half, half)
            store_o(ITERS - 1, 1)
            sp.wait_ge(o_even_free, 16 * (ITERS + 1))
            sp.wait_ge(o_odd_free, 16 * (ITERS + 1))

            with sp.Fori(1, X_G // 2) as i:
                for half in (0, 1):
                    d = 2 * i + half
                    sp.wait_ge(o_turned, 2 * (d - 1))
                    load_og(half, i)
                    sp.wait_ge(x1_ready, GT * (d - 1))
                    load_x2(d, half)

            def f_store(d):
                sp.wait_ge(f_added, GT * (d + 1))
                sp.dma_start(out.rearrange("(g t p) f -> g p t f", p=P, t=GT)[d],
                             x1[:, bass.ds(GT * d, GT), :]).then_inc(stored, 16)

            with sp.Fori(0, X_G) as d:
                f_store(d)
            sp.wait_ge(stored, 16 * X_G)

        @block.gpsimd
        def _(pool):
            nc.gpsimd.memset(ident[:, :], 0.0).then_inc(consts, 1)
            nc.gpsimd.memset(fold[:, :], 0.0).then_inc(consts, 1)
            nc.gpsimd.memset(ones[:, :], 1.0).then_inc(consts, 1)
            pool.wait_ge(consts, 3)
            nc.gpsimd.affine_select(out=ident[:, :], in_=ident[:, :], compare_op=ALU.not_equal, fill=1.0,
                                    base=0, pattern=[[-1, P]], channel_multiplier=1).then_inc(consts, 1)
            nc.gpsimd.affine_select(out=fold[:, :], in_=fold[:, :], compare_op=ALU.not_equal, fill=1.0,
                                    base=0, pattern=[[-1, HD]], channel_multiplier=1).then_inc(consts, 1)
            pool.wait_ge(consts, 5)
            nc.gpsimd.affine_select(out=fold[:, :], in_=fold[:, :], compare_op=ALU.not_equal, fill=1.0,
                                    base=-HD, pattern=[[-1, HD]], channel_multiplier=1).then_inc(consts, 1)

            def k_low(v, v_it, hh, p, own_sums):
                a, b = slice(HD * hh, HD * hh + HD), slice(HD * (1 - hh), HD * (1 - hh) + HD)
                c = slice(*PIECES[p])
                wait(pool, summed_g, own_sums)
                pool.wait_ge(k_hi, 4 * v + (p + 1))
                nc.gpsimd.tensor_tensor(k1[b, hh, c], kt4[a, v_it % PAIRS, c], k1[a, hh, c].bitcast(F32),
                                        ALU.subtract).then_inc(k_lo, 1)
                pool.wait_ge(k_lo, 4 * v + (p + 1))

            def fold_halves(w):
                pool.wait_ge(summed_g, SUMS_G * w + (SUMS_G - 2))
                nc.gpsimd.tensor_tensor(sums[:, 1, 0:QB], sums[:, 1, 0:QB], sums[:, 1, QB:], ALU.add)\
                    .then_inc(summed_g, 1)

            def take_sums(w):
                pool.wait_ge(summed_v, SUMS_V * (w + 1))
                pool.wait_ge(summed_g, SUMS_G * w + (SUMS_G - 1))
                nc.gpsimd.tensor_tensor(sums[:, 1, 0:QB], sums[:, 1, 0:QB], sums[:, 0, 0:QB], ALU.add)\
                    .then_inc(summed_g, 1)

            for p in range(4):
                k_low(0, 0, 0, p, 0)
            pool.wait_ge(q1_ready, 1)
            nc.gpsimd.tensor_tensor(q2[0:HD, 0, :], qt_first[0:HD], q1[0:HD, 0, :].bitcast(F32), ALU.subtract)\
                .then_inc(q2_ready, 1)
            pool.wait_ge(q2_ready, 1)
            for p in range(2):
                k_low(1, 0, 1, p, 0)

            def c_unit(it, hh, first, last):
                w = 2 * it + hh
                w1, it1, hh1 = ahead(it, hh, 1)
                w2, it2, hh2 = ahead(it, hh, 2)
                if not (first and hh == 0):
                    take_sums(w - 1)
                if not (last and hh == 1):
                    k_low(w1, it1, hh1, 2, SUMS_G * w)
                    k_low(w1, it1, hh1, 3, SUMS_G * w)
                for s in range(3, NP, 2):
                    pool.wait_ge(exped, NP * w + (s + 1))
                    if s == 3:
                        wait(pool, folded, w)
                        a = pt[:, pt_slot(hh, 1)]
                    else:
                        pool.wait_ge(summed_g, SUMS_G * w + pe_sum_index(s))
                        a = sums[:, 1]
                    nc.gpsimd.tensor_tensor(sums[:, 1], a, pt[:, pt_slot(hh, s)], ALU.add).then_inc(summed_g, 1)
                    if s in (5, 9) and not last:
                        k_low(w2, it2, hh2, (s - 5) // 4, SUMS_G * w + (pe_sum_index(s) + 1))
                fold_halves(w)

            c_steps(pool, c_unit)
            take_sums(UNIT_N - 1)
            pool.wait_ge(bo_loaded, 16)

            def d_body(i, slot):
                pool.wait_ge(x2_loaded[slot], 16 * (i + 1))
                for t in range(GT):
                    ins = nc.gpsimd.tensor_tensor(xb[:, slot, t], xb[:, slot, t], bo, ALU.add)
                ins.then_inc(xb_ready, 1)

            with pool.Fori(0, X_G // 2) as i:
                for s in (0, 1):
                    d_body(i, s)

        @block.scalar
        def _(act):
            def b_front(g, slot, loads):
                wait(act, kq_done, FC * (g - 1))
                for c in range(FC):
                    if c % 2 == 0:
                        act.wait_ge(transposed, 2 * g + (c // 2 + 1))
                    nc.scalar.activation(nt[:, slot, c], ps[:, c // 2, (c % 2) * GW:(c % 2 + 1) * GW],
                                         ACT.Identity, bias=be1[:, c:c + 1], scale=g1[:, c:c + 1])\
                        .then_inc(nt_ready, 1)

            def b_back(g, slot, *block_half):
                is_ctx = isinstance(g, int) and g < CTX_G or not isinstance(g, int) and not block_half
                if not is_ctx:
                    if isinstance(g, int) and g == CTX_G:
                        act.wait_ge(v_evac, GT * CTX_G)
                    blk, half = x_group(g, block_half)
                    wait(act, q_stored[half], 16 * blk)
                for c in range(FC):
                    act.wait_ge(kq_done, FC * g + (c + 1))
                    if is_ctx:
                        dst = kt4[:, c, bass.ds(g * GW, GW)]
                    else:
                        dst = wo_qo[:, c, half * GW:(half + 1) * GW]
                    nc.scalar.activation(dst, ps[:, 2 + c, 0:GW], ACT.Identity,
                                         bias=(bk if is_ctx else bq)[:, c:c + 1]).then_inc(kq_evac, 1)

            act.wait_ge(setup_loaded, 16 * 9)
            for c, cols_c in ((0, slice(0, KEYS)), (1, slice(KEYS, KPAD))):
                n = cols_c.stop - cols_c.start
                ins = nc.scalar.activation(k2[HD:HD + 2, cols_c], k2_cols[HD:HD + 2, c:c + 1].to_broadcast([2, n]),
                                           ACT.Copy)
            ins.then_inc(k2_rows_set, 1)

            def own(hh):
                return slice(HD * hh, HD * hh + HD), slice(HD * (1 - hh), HD * (1 - hh) + HD)

            def k_high(v_it, hh, p):
                a, _ = own(hh)
                c = slice(*PIECES[p])
                nc.scalar.activation(k1[a, hh, c], kt4[a, v_it % PAIRS, c], ACT.Copy).then_inc(k_hi, 1)

            def k2_high(v_it, hh, p):
                a, _ = own(hh)
                c = slice(*PIECES[p])
                nc.scalar.activation(k2[0:HD, c], kt4[a, v_it % PAIRS, c], ACT.Copy).then_inc(k2_ready, 1)

            def q_high(dst, hh, done, src=qt_sb):
                a, b = own(hh)
                nc.scalar.activation(dst[a], src[a, :], ACT.Copy)
                nc.scalar.activation(dst[b], src[a, :], ACT.Copy).then_inc(done, 1)

            def shift(v, slot):
                act.wait_ge(max_turned, v + 1)
                nc.scalar.activation(q2[HD:HD + 1, slot, :], ps[0:1, 7, :], ACT.Copy, scale=-1.0)\
                    .then_inc(shift_ready, 1)

            def c_first(g):
                if g == CTX_G:
                    act.wait_ge(kq_evac, FC * (CTX_G + 1))
                    for p in range(4):
                        k_high(0, 0, p)
                if g == CTX_G + 1:
                    act.wait_ge(kq_evac, FC * (CTX_G + 2))
                    act.wait_ge(q2_ones_set, 1)
                    q_high(q_max[:, :], 0, qm_ready, qt_first)
                    q_high(q1[:, 0], 0, q1_ready, qt_first)
                    for p in range(3):
                        k_high(0, 1, p)
                    act.wait_ge(q2_ready, 1)
                if g == NG - 2:
                    for p in range(3):
                        k2_high(0, 0, p)
                    act.wait_ge(max_done, NM)
                    act.wait_ge(qt_loaded, 16)
                    q_high(q_max[:, :], 1, qm_ready)
                if g == NG - 1:
                    shift(0, 0)

            b_steps(act, b_front, b_back, c_first)

            def take_half(w):
                act.wait_ge(pv_done, NP * (w + 1))
                wait(act, folded, w)
                nc.scalar.activation(o_half[:, :], ps[:, 6, :], ACT.Copy).then_inc(half_ready, 1)

            def exp_pair(it, hh, s, first):
                w = 2 * it + hh
                act.wait_ge(scored, NP * w + (s + 1))
                if not (first and NP * hh + s < PT_SLOTS):
                    w_b, s_b = pt_user_before(w, hh, s)
                    act.wait_ge(pv_done, NP * w_b + (s_b + 1))
                    if s_b % 2:
                        act.wait_ge(summed_g, SUMS_G * w_b + (pe_sum_index(s_b) + 1))
                    else:
                        act.wait_ge(summed_v, SUMS_V * w_b + (pe_sum_index(s_b) + 1))
                b = 2 * ((NP * hh + s) % 2)
                nc.scalar.activation(pt[:, pt_slot(hh, s)], ps[:, b:b + 2, :].rearrange("p a b -> p (a b)"),
                                     ACT.Exp, scale=SCALE).then_inc(exped, 1)

            def c_unit(it, hh, first, last):
                w = 2 * it + hh
                w1, it1, hh1 = ahead(it, hh, 1)
                w2, it2, hh2 = ahead(it, hh, 2)
                next1 = not (last and hh == 1)
                next2 = not last
                for s in range(NP):
                    if s == NP - 1 and next1:
                        shift(w1, hh1)
                    exp_pair(it, hh, s, first)
                    if s == 0:
                        if not (first and hh == 0):
                            take_half(w - 1)
                        k2_high(it, hh, 3)
                        if next1:
                            k_high(it1, hh1, 3)
                    if s == 1 and next1:
                        act.wait_ge(qt_loaded, 16 * (it1 + 1))
                        q_high(q1[:, hh1], hh1, q1_ready)
                    for p, (s_k, s_k2) in enumerate(((5, 6), (9, 10), (12, 12))):
                        if s == s_k and next2:
                            k_high(it2, hh2, p)
                        if s == s_k2 and next1:
                            k2_high(it1, hh1, p)
                    if s == 11 and next2:
                        act.wait_ge(max_done, NM * (w1 + 1))
                        act.wait_ge(qt_loaded, 16 * (it2 + 1))
                        q_high(q_max[:, :], hh2, qm_ready)

            c_steps(act, c_unit)
            take_half(UNIT_N - 1)

            def turn(d, slot):
                wait(act, y_done, GT * (d - 1))
                for k in range(2):
                    act.wait_ge(o_turned, 2 * d + (k + 1))
                    nc.scalar.activation(ot[:, slot, 2 * k:2 * k + 2].rearrange("p c k -> p (c k)"),
                                         ps[:, k, :], ACT.Copy).then_inc(ot_ready, 1)

            def turn2(d, slot):
                wait(act, u_done, d - 1)
                for c in range(FC):
                    if c % 2 == 0:
                        act.wait_ge(n2_turned, 2 * d + (c // 2 + 1))
                    nc.scalar.activation(nt[:, slot, c], ps[:, 4 + c // 2, (c % 2) * GW:(c % 2 + 1) * GW],
                                         ACT.Identity, bias=be2[:, c:c + 1], scale=g2[:, c:c + 1])\
                        .then_inc(n2t_ready, 1)

            def finish(d, slot):
                act.wait_ge(u_done, d + 1)
                nc.scalar.activation(u_all[:, bass.ds(d * GW, GW)], ps[0:SD, 6, 0:GW], ACT.Identity,
                                     bias=cu[:, 0:1]).then_inc(u_ready, 1)

            d_steps(act, turn, lambda d, slot, t: None, turn2, finish)
            act.wait_ge(c_cleared, 1)
            for rows in (slice(0, SD), slice(SD, 2 * SD)):
                nc.scalar.activation(c1[rows], c_aug[0:SD, :], ACT.Copy)
            nc.scalar.activation(c2[SD:SD + 1], c_aug[SD:SD + 1, :], ACT.Copy).then_inc(c_hi, 1)

            def scan_steps(first):
                with act.Fori(0, LCH // 2) as i:
                    for s in (0, 1):
                        for h, c in scan_halves():
                            act.wait_ge(z_done, 2 * (2 * i + (first + s)) + (h + 1))
                            nc.scalar.activation(sg[:, c], ps[SD:2 * SD, h, 0:NCH // 2], ACT.Silu)\
                                .then_inc(silu_done, 1)

            scan_steps(0)
            scan_steps(LCH)
            act.wait_ge(flag_ready, 1)
            good = act.value_load(flag[0:1, 0:1], min_val=0, max_val=1)
            with act.If(good == 0):
                with act.Fori(0, T) as n:
                    act.wait_ge(seq_z, n + 1)
                    nc.scalar.activation(sg[:, 0:1], ps[SD:2 * SD, 0, 0:1], ACT.Silu).then_inc(seq_silu, 1)
                act.wait_ge(seq_st, T)

            def f_high(d, slot):
                wait(act, f_done, GT * (d - 1))
                src = s_all[:, bass.ds(d * GW + 1, GW)]
                nc.scalar.activation(s1[0:SD, slot], src, ACT.Copy)
                nc.scalar.activation(s2[0:SD, slot], src, ACT.Copy).then_inc(s_hi, 1)

            for s in (0, 1):
                f_high(s, s)
            with act.Fori(1, X_G // 2) as i:
                for s in (0, 1):
                    f_high(2 * i + s, s)

        @block.vector
        def _(dve):
            def layernorm(n, src, dst, dst_free, done):
                step = [LN_STEPS * n, 0]

                def link(ins):
                    step[1] += 1
                    ins.then_inc(ln_step, 1)
                    wait_apart(dve, ln_step, step[0] + step[1], tick)

                for t in range(GT):
                    ins = nc.vector.bn_stats(stats[:, t, :], src(t))
                link(ins)
                for t in range(GT):
                    ins = nc.vector.bn_aggr(mv[:, t, :], stats[:, t, :])
                link(ins)
                link(nc.vector.tensor_scalar(ve[:, :], mv[:, :, 1], EPS, None, ALU.add))
                link(nc.vector.tensor_scalar(yi[:, :], ve[:, :].bitcast(I32), 1, None,
                                             ALU.logical_shift_right))
                link(nc.vector.tensor_scalar(ya[:, :].bitcast(I32), yi[:, :], -1, 0x5F3759DF,
                                             ALU.mult, ALU.add))
                for _ in range(3):
                    link(nc.vector.tensor_tensor(yb[:, :], ya[:, :], ya[:, :], ALU.mult))
                    link(nc.vector.scalar_tensor_tensor(out=yb[:, :], in0=yb[:, :], scalar=-0.5,
                                                        in1=ve[:, :], op0=ALU.mult, op1=ALU.mult))
                    link(nc.vector.scalar_tensor_tensor(out=ya[:, :], in0=yb[:, :], scalar=1.5,
                                                        in1=ya[:, :], op0=ALU.add, op1=ALU.mult))
                assert step[1] == LN_STEPS
                dst_free()
                for t in range(GT):
                    ins = nc.vector.tensor_scalar(dst(t), src(t), mv[:, t, 0:1], ya[:, t:t + 1],
                                                  ALU.subtract, ALU.mult)
                ins.then_inc(done, 1)

            dve.wait_ge(setup_mm, 3)
            nc.vector.tensor_copy(w_u[:, :, :].rearrange("p c s -> p (c s)"), ps[:, 0, 0:FC * SD])\
                .then_inc(setup_ev, 1)
            nc.vector.tensor_copy(cu[:, :], ps[0:SD, 1, 0:1]).then_inc(setup_ev, 1)
            nc.vector.tensor_scalar(mean[:, :], ps[0:SD, 2, 0:1], 1.0 / KEYS, None, ALU.mult)\
                .then_inc(setup_ev, 1)
            dve.wait_ge(setup_mm, 4)
            nc.vector.tensor_tensor(c_aug[SD:SD + 1, :], ps[0:1, 3, :], bp, ALU.add)\
                .then_inc(setup_ev, 1)

            def b_front(g, slot, loads):
                wait_apart(dve, xs_loaded[slot], 16 * loads, tick)
                layernorm(g, lambda t: xs[:, slot, t, :], lambda t: xs[:, slot, t, :], lambda: None, normed)

            def b_back(g, slot, *block_half):
                if isinstance(g, int) and g >= CTX_G or block_half:
                    return
                for t in range(GT):
                    dve.wait_ge(v_done, GT * g + (t + 1))
                    nc.vector.tensor_tensor(v[:, GT * g + t, :], ps[:, 6 + t, :], bv, ALU.add)\
                        .then_inc(v_evac, 1)

            nc.vector.memset(q2[HD:HD + 2, :, :].bitcast(F32), 1.0).then_inc(q2_ones_set, 1)

            def own(hh):
                return slice(HD * hh, HD * hh + HD), slice(HD * (1 - hh), HD * (1 - hh) + HD)

            def q_low(v, hh):
                a, _ = own(hh)
                dve.wait_ge(q1_ready, v + 1)
                nc.vector.tensor_tensor(q2[0:HD, hh, :], qt_sb[a, :], q1[a, hh, :].bitcast(F32),
                                        ALU.subtract).then_inc(q2_ready, 1)

            def take_max(v, m):
                dve.wait_ge(max_done, NM * v + (m + 1))
                if m < NM - 1:
                    nc.vector.tensor_reduce(mx_part[:, m % QT_N, m // QT_N:m // QT_N + 1],
                                            ps[:, 4:6, :].rearrange("p a b -> p (a b)"), AX_X, ALU.max)\
                        .then_inc(max_taken, 1)
                else:
                    n = KEYS - TAIL
                    nc.vector.tensor_reduce(mx_part[:, 0:2, 3], ps[:, 4, 0:2 * n].rearrange("p (q k) -> p q k", q=2),
                                            AX_X, ALU.max)
                    nc.vector.tensor_reduce(mx_part[:, 2:4, 3], ps[:, 5, 0:2 * n].rearrange("p (q k) -> p q k", q=2),
                                            AX_X, ALU.max).then_inc(max_taken, 1)

            def row_max(v, parts=mx_part):
                dve.wait_ge(max_taken, NM * v)
                nc.vector.tensor_reduce(mx[:, :], parts[:, :, :], AX_X, ALU.max).then_inc(max_ready, 1)

            def c_first(g):
                if g == CTX_G + 1:
                    dve.sem_inc(first_free, 1)
                if g == NG - 2:
                    dve.wait_ge(max_done, NM)
                    n = KEYS - TAIL
                    for b in (0, 1):
                        ins = nc.vector.tensor_reduce(mx_first[:, 2 * b:2 * b + 2, 6],
                                                      ps[:, 6 + b, 0:2 * n].rearrange("p (q k) -> p q k", q=2),
                                                      AX_X, ALU.max)
                    ins.then_inc(first_free, 1)
                    dve.wait_ge(first_free, NM + 1)
                    row_max(0, mx_first)

            def c_first_maxima(i, s):
                dve.wait_ge(max_done, 2 * i + (s + 1))
                nc.vector.tensor_reduce(mx_first[:, 2 * s:2 * s + 2, bass.ds(i, 1)], ps[:, 6:8, :], AX_X, ALU.max)\
                    .then_inc(first_free, 1)

            b_steps(dve, b_front, b_back, c_first, inside=c_first_maxima)

            def fold_sum(w):
                dve.wait_ge(summed_v, SUMS_V * w + (SUMS_V - 1))
                nc.vector.tensor_tensor(sums[:, 0, 0:QB], sums[:, 0, 0:QB], sums[:, 0, QB:], ALU.add)\
                    .then_inc(summed_v, 1)

            def add_pair(w, hh, s):
                dve.wait_ge(exped, NP * w + (s + 1))
                if s == 2:
                    wait(dve, summed_g, SUMS_G * w)
                    a = pt[:, pt_slot(hh, 0)]
                else:
                    dve.wait_ge(summed_v, SUMS_V * w + pe_sum_index(s))
                    a = sums[:, 0]
                nc.vector.tensor_tensor(sums[:, 0], a, pt[:, pt_slot(hh, s)], ALU.add).then_inc(summed_v, 1)

            for free in (o_even_free, o_odd_free):
                dve.sem_inc(free, 16)

            def scale_out(w, w_it, hh):
                dve.wait_ge(folded, w + 1)
                nc.vector.reciprocal(rden[:, :], ps[:, 7, QT_N * HD:QT_N * HD + QT_N]).then_inc(rden_ready, 1)
                dve.wait_ge(rden_ready, w + 1)
                wait(dve, (o_even_free, o_odd_free)[hh], 16 * (w_it + 1))
                nc.vector.tensor_tensor(o_out[:, hh], ps[:, 7, 0:QT_N * HD].rearrange("p (q d) -> p q d", q=QT_N),
                                        rden[:, :].rearrange("p (q o) -> p q o", o=1).to_broadcast([P, QT_N, HD]),
                                        ALU.mult).then_inc(o_scaled, 1)


            def c_unit(it, hh, first, last):
                w = 2 * it + hh
                w1, it1, hh1 = ahead(it, hh, 1)
                next1 = not (last and hh == 1)
                before = not (first and hh == 0)
                _, it_b, hh_b = ahead(it, hh, -1)
                for s in range(NP):
                    if next1:
                        for m in MAX_AT[s][:1]:
                            take_max(w1, m)
                        if s == NP - 2:
                            row_max(w1)
                    if s == 0:
                        if before:
                            add_pair(w - 1, hh_b, NP - 1)
                            fold_sum(w - 1)
                    if s == 2 and next1:
                        q_low(w1, hh1)
                    if s == 4 and before:
                        scale_out(w - 1, it_b, hh_b)
                    if s >= 3 and s % 2:
                        add_pair(w, hh, s - 1)
                    if next1:
                        for m in MAX_AT[s][1:]:
                            take_max(w1, m)

            c_steps(dve, c_unit)
            add_pair(UNIT_N - 1, 1, NP - 1)
            fold_sum(UNIT_N - 1)
            scale_out(UNIT_N - 1, ITERS - 1, 1)

            def project(d, slot, t):
                dve.wait_ge(xb_ready, d + 1)
                dve.wait_ge(y_done, GT * d + (t + 1))
                nc.vector.tensor_tensor(x1[:, GT * d + t, :], ps[:, 2 + t, :], xb[:, slot, t], ALU.add)\
                    .then_inc(x1_ready, 1)
                if t < GT - 1:
                    return
                wait_apart(dve, x1_ready, GT * (d + 1), tick)
                layernorm(d + NG, lambda t: x1[:, GT * d + t, :], lambda t: xn[:, t, :],
                          lambda: wait(dve, n2_turned, 2 * d), normed2)

            def nothing(d, slot):
                pass

            dve.wait_ge(scored, NP * UNIT_N)
            nc.vector.memset(c2[SD:MOD_LO + 1].bitcast(F32), 0.0)
            nc.vector.memset(s2[SD:MOD_LO + 1].bitcast(F32), 1.0).then_inc(c_cleared, 1)
            d_steps(dve, nothing, project, nothing, nothing)
            dve.wait_ge(c_hi, 1)
            nc.vector.tensor_tensor(c2[0:SD], c_aug[0:SD, :], c1[0:SD].bitcast(F32), ALU.subtract)
            nc.vector.tensor_tensor(c2[MOD_LO:MOD_LO + 1], c_aug[SD:SD + 1, :], c2[SD:SD + 1].bitcast(F32),
                                    ALU.subtract).then_inc(c_ready, 1)

            dve.wait_ge(u_ready, X_G)
            for h, c in scan_halves():
                nc.vector.memset(st[:, 0, c], 0.0).then_inc(st_ready, 1)

            with dve.Fori(0, LCH // 2) as i:
                for s in (0, 1):
                    for h, c in scan_halves():
                        dve.wait_ge(silu_done, 2 * (2 * i + s) + (h + 1))
                        nc.vector.tensor_tensor(st[:, 1 - s, c], sg[:, c], u_steps[:, 2 * i + s, c], ALU.add)\
                            .then_inc(st_ready, 1)
            dve.wait_ge(st_ready, 2 * (LCH + 1))
            nc.vector.tensor_copy(end1, st[:, 0]).then_inc(cmp_step, 1)
            nc.vector.memset(s_all[:, 0:1], 0.0)
            for h, c in scan_halves():
                a = max(c.start, 1)
                nc.vector.tensor_copy(s_from[:, 0, a:c.stop], st[:, 0, a - 1:c.stop - 1]).then_inc(st_ready, 1)
            with dve.Fori(0, LCH // 2) as i:
                for s in (0, 1):
                    for h, c in scan_halves():
                        dve.wait_ge(silu_done, 2 * (2 * i + (LCH + s)) + (h + 1))
                        nc.vector.tensor_tensor(s_to[:, 2 * i + s, c], sg[:, c], u_steps[:, 2 * i + s, c],
                                                ALU.add).then_inc(st_ready, 1)
            dve.wait_ge(st_ready, 2 * (2 * LCH + 2))
            ends = s_to[:, LCH - 1, :]
            nc.vector.tensor_tensor(diff, ends, end1, ALU.subtract).then_inc(cmp_step, 1)
            dve.wait_ge(cmp_step, 2)
            nc.vector.tensor_tensor(sq[:, 0], diff, diff, ALU.mult)
            nc.vector.tensor_tensor(sq[:, 1], ends, ends, ALU.mult).then_inc(cmp_step, 1)
            dve.wait_ge(sums_done, 1)
            nc.vector.tensor_copy(e_row, ps[0:1, 3, 0:NCH]).then_inc(cmp_step, 1)
            dve.wait_ge(cmp_step, 4)
            nc.vector.scalar_tensor_tensor(out=lhs_row, in0=e_row, scalar=-TOL2, in1=ps[0:1, 2, 0:NCH],
                                           op0=ALU.mult, op1=ALU.add).then_inc(cmp_step, 1)
            dve.wait_ge(cmp_step, 5)
            nc.vector.tensor_scalar(ok_row, lhs_row, 0.0, None, ALU.is_le).then_inc(cmp_step, 1)
            dve.wait_ge(cmp_step, 6)
            nc.vector.tensor_reduce(flag_f[:, 0:1], ok_row, AX_X, ALU.min).then_inc(cmp_step, 1)
            dve.wait_ge(cmp_step, 7)
            nc.vector.tensor_copy(flag[:, :], flag_f[:, 0:1]).then_inc(flag_ready, 1)
            dve.wait_ge(flag_ready, 1)
            good = dve.value_load(flag[0:1, 0:1], min_val=0, max_val=1)
            with dve.If(good == 0):
                with dve.Fori(0, T) as n:
                    dve.wait_ge(seq_silu, n + 1)
                    nc.vector.tensor_tensor(s_all[:, bass.ds(n + 1, 1)], sg[:, 0:1], u_all[:, bass.ds(n, 1)],
                                            ALU.add).then_inc(seq_st, 1)
                dve.wait_ge(seq_st, T)

            def f_low(d, slot):
                dve.wait_ge(s_hi, d + 1)
                nc.vector.tensor_tensor(s1[SD:2 * SD, slot], s_all[:, bass.ds(d * GW + 1, GW)],
                                        s1[0:SD, slot].bitcast(F32), ALU.subtract).then_inc(s_lo, 1)

            def f_add(d, slot):
                for t in range(GT):
                    dve.wait_ge(f_done, GT * d + (t + 1))
                    nc.vector.tensor_tensor(x1[:, GT * d + t, :], ps[:, 4 + 2 * slot + t, :],
                                            x1[:, GT * d + t, :], ALU.add).then_inc(f_added, 1)

            f_low(0, 0)
            f_low(1, 1)
            with dve.Fori(0, X_G // 2 - 1) as i:
                for s in (0, 1):
                    f_add(2 * i + s, s)
                    f_low(2 * i + (2 + s), s)
            for s in (0, 1):
                f_add(X_G - 2 + s, s)

        @block.tensor
        def _(pe):
            mm = nc.tensor.matmul
            pe.wait_ge(setup_loaded, 16 * 9)
            pe.wait_ge(consts, 6)
            for m in range(FC):
                for k in range(FC):
                    ins = mm(ps[:, 0, m * SD:(m + 1) * SD], win_sb[:, k, m * P:(m + 1) * P], b_sb[:, k, :],
                             start=(k == 0), stop=(k == FC - 1))
            ins.then_inc(setup_mm, 1)
            for k in range(FC):
                ins = mm(ps[0:SD, 1, 0:1], b_sb[:, k, :], bin_[:, k:k + 1], start=(k == 0), stop=(k == FC - 1))
            ins.then_inc(setup_mm, 1)
            for t in range(KT_TILES):
                ins = mm(ps[0:SD, 2, 0:1], cb_sb[:, t, :], ones[:, :], start=(t == 0), stop=(t == KT_TILES - 1))
            ins.then_inc(setup_mm, 1)
            pe.wait_ge(setup_ev, 3)
            mm(ps[0:1, 3, :], mean[:, :], wp_sb, start=True, stop=True).then_inc(setup_mm, 1)
            pe.wait_ge(setup_ev, 4)

            def b_front(g, slot, loads):
                pe.wait_ge(normed, g + 1)
                wait(pe, nt_ready, FC * g)
                for c in range(FC):
                    for t in range(GT):
                        ins = nc.tensor.transpose(ps[:, c // 2, (c % 2) * GW + t * P:(c % 2) * GW + (t + 1) * P],
                                                  xs[:, slot, t, c * P:(c + 1) * P], ident[:, :])
                    if c % 2:
                        ins.then_inc(transposed, 1)

            def b_back(g, slot, *block_half):
                is_ctx = isinstance(g, int) and g < CTX_G or not isinstance(g, int) and not block_half
                pe.wait_ge(nt_ready, FC * (g + 1))
                if isinstance(g, int) and g == 0:
                    pe.wait_ge(w_loaded, 16)
                if is_ctx:
                    for t in range(GT):
                        wait(pe, v_evac, GT * (g - 1) + (t + 1))
                        for k in range(FC):
                            ins = mm(ps[:, 6 + t, :], nt[:, slot, k, t * P:(t + 1) * P], w3[:, 2, k, :],
                                     start=(k == 0), stop=(k == FC - 1))
                        ins.then_inc(v_done, 1)
                for c in range(FC):
                    wait(pe, kq_evac, FC * (g - 1) + (c + 1))
                    for k in range(FC):
                        ins = mm(ps[:, 2 + c, 0:GW], w3[:, 1 if is_ctx else 0, k, c * P:(c + 1) * P],
                                 nt[:, slot, k, :], start=(k == 0), stop=(k == FC - 1))
                    ins.then_inc(kq_done, 1)

            def maxima(v, hh, m):
                if m % QT_N == 0:
                    pe.wait_ge(k_lo, 4 * v + (m // QT_N + 1))
                if m == 0:
                    pe.wait_ge(qm_ready, v + 1)
                wait(pe, max_taken, NM * (v - 1) + m)
                if m < NM - 1:
                    a, q = 1024 * (m // QT_N), m % QT_N
                    for o in (0, 1):
                        ins = mm(ps[:, 4 + o, :], q_max[:, q * P:(q + 1) * P],
                                 k1[:, hh, a + 512 * o:a + 512 * (o + 1)], start=True, stop=True)
                else:
                    n = KEYS - TAIL
                    for q in range(QT_N):
                        ins = mm(ps[:, 4 + q // 2, (q % 2) * n:(q % 2 + 1) * n], q_max[:, q * P:(q + 1) * P],
                                 k1[:, hh, TAIL:KEYS], start=True, stop=True)
                ins.then_inc(max_done, 1)

            def turn_max(v):
                pe.wait_ge(max_ready, v + 1)
                wait(pe, o_scaled, v - 1)
                for q in range(QT_N):
                    ins = nc.tensor.transpose(ps[0:1, 7, q * P:(q + 1) * P], mx[:, q:q + 1], ident[:, :])
                ins.then_inc(max_turned, 1)

            def c_first(g):
                if g == CTX_G + 1:
                    pe.wait_ge(v_evac, GT * CTX_G)
                    pe.wait_ge(k_lo, 4)
                    pe.wait_ge(qm_ready, 1)
                if g == NG - 2:
                    pe.wait_ge(first_free, NM)
                    n = KEYS - TAIL
                    for q in range(QT_N):
                        ins = mm(ps[:, 6 + q // 2, (q % 2) * n:(q % 2 + 1) * n], q_max[:, q * P:(q + 1) * P],
                                 k1[:, 0, TAIL:KEYS], start=True, stop=True)
                    ins.then_inc(max_done, 1)
                if g == NG - 1:
                    turn_max(0)

            def c_first_maxima(i, s):
                pe.wait_ge(first_free, 2 * i + (s + 1))
                for q in (0, 1):
                    ins = mm(ps[:, 6 + q, :], q_max[:, (2 * s + q) * P:(2 * s + q + 1) * P],
                             k1[:, 0, bass.ds(512 * i, 512)], start=True, stop=True)
                ins.then_inc(max_done, 1)

            b_steps(pe, b_front, b_back, c_first, before=c_first_maxima)

            def scores(w, hh, s):
                for p, s_p in enumerate((0, 4, 8, 12)):
                    if s == s_p:
                        pe.wait_ge(k2_ready, 4 * w + (p + 1))
                if s == 0:
                    pe.wait_ge(q1_ready, w + 1)
                    pe.wait_ge(q2_ready, w + 1)
                    pe.wait_ge(shift_ready, w + 1)
                wait(pe, exped, NP * w + (s - 1))
                b = 2 * ((NP * hh + s) % 2)
                for i in (0, 1):
                    k = slice((2 * s + i) * P, (2 * s + i + 1) * P)
                    mm(ps[:, b + i, :], k1[:, hh, k], q1[:, hh, :], start=True, stop=False)
                    ins = mm(ps[:, b + i, :], k2[0:HD + 2, k], q2[:, hh, :], start=False, stop=True)
                ins.then_inc(scored, 1)

            def pv(w, w_it, hh, s):
                if s == 0:
                    pe.wait_ge((v_even_loaded, v_odd_loaded)[hh], 16 * (w_it + 1))
                    wait(pe, half_ready, w)
                pe.wait_ge(exped, NP * w + (s + 1))
                for i in (0, 1):
                    r = HD * i
                    ins = mm(ps[r:r + HD, 6, :], v_head[:, hh, 2 * s + i, :],
                             pt[:, pt_slot(hh, s), i * QB:(i + 1) * QB], start=(s == 0), stop=(s == NP - 1))
                ins.then_inc(pv_done, 1)

            def fold_out(w):
                pe.wait_ge(half_ready, w + 1)
                pe.wait_ge(summed_g, SUMS_G * (w + 1))
                wait(pe, o_scaled, w)
                for q in range(QT_N):
                    mm(ps[:, 7, QT_N * HD + q:QT_N * HD + q + 1], sums[:, 1, q * P:(q + 1) * P],
                       ones[:, :], start=True, stop=True)
                for q in range(QT_N):
                    ins = mm(ps[:, 7, q * HD:(q + 1) * HD], o_half[:, q * P:(q + 1) * P], fold[:, :],
                             start=True, stop=True)
                ins.then_inc(folded, 1)

            pe.wait_ge(kq_evac, FC * NG)
            pe.wait_ge(v_evac, GT * CTX_G)

            def c_unit(it, hh, first, last):
                w = 2 * it + hh
                w1, it1, hh1 = ahead(it, hh, 1)
                next1 = not (last and hh == 1)
                before = not (first and hh == 0)
                for s in range(NP):
                    scores(w, hh, s)
                    if s == NP - 1 and next1:
                        turn_max(w1)
                    if next1:
                        for m in MAX_AT[s][:1]:
                            maxima(w1, hh1, m)
                    if s > 0:
                        pv(w, it, hh, s - 1)
                    elif before:
                        pv(w - 1, ahead(it, hh, -1)[1], 1 - hh, NP - 1)
                    if s == 3 and before:
                        fold_out(w - 1)
                    if next1:
                        for m in MAX_AT[s][1:]:
                            maxima(w1, hh1, m)

            c_steps(pe, c_unit)
            pv(UNIT_N - 1, ITERS - 1, 1, NP - 1)
            fold_out(UNIT_N - 1)

            def turn(d, slot):
                pe.wait_ge(og_loaded[slot], 8 * GT * (d - slot) + 16 * GT)
                wait(pe, ot_ready, 2 * d)
                for c in range(FC):
                    for t in range(GT):
                        ins = nc.tensor.transpose(ps[:, c // 2, (c % 2) * GW + t * P:(c % 2) * GW + (t + 1) * P],
                                                  og[:, slot, t, 2 * c:2 * c + 2].rearrange("p h d -> p (h d)"),
                                                  ident[:, :])
                    if c % 2:
                        ins.then_inc(o_turned, 1)

            def project(d, slot, t):
                pe.wait_ge(ot_ready, 2 * (d + 1))
                wait(pe, x1_ready, GT * (d - 1) + (t + 1))
                for k in range(FC):
                    ins = mm(ps[:, 2 + t, :], ot[:, slot, k, t * P:(t + 1) * P], w_o[:, k, :],
                             start=(k == 0), stop=(k == FC - 1))
                ins.then_inc(y_done, 1)

            def turn2(d, slot):
                pe.wait_ge(normed2, d + 1)
                wait(pe, n2t_ready, FC * d)
                for c in range(FC):
                    for t in range(GT):
                        ins = nc.tensor.transpose(
                            ps[:, 4 + c // 2, (c % 2) * GW + t * P:(c % 2) * GW + (t + 1) * P],
                            xn[:, t, c * P:(c + 1) * P], ident[:, :])
                    if c % 2:
                        ins.then_inc(n2_turned, 1)

            def finish(d, slot):
                pe.wait_ge(n2t_ready, FC * (d + 1))
                wait(pe, u_ready, d)
                for k in range(FC):
                    ins = mm(ps[0:SD, 6, 0:GW], w_u[:, k, :], nt[:, slot, k, :],
                             start=(k == 0), stop=(k == FC - 1))
                ins.then_inc(u_done, 1)

            pe.wait_ge(wo_loaded, 16)
            pe.wait_ge(o_scaled, UNIT_N)
            d_steps(pe, turn, project, turn2, finish)

            pe.wait_ge(at_loaded, 32)

            def scan_steps(first, states):
                with pe.Fori(0, LCH // 2) as i:
                    for s in (0, 1):
                        for h, c in scan_halves():
                            n = 2 * (2 * i + (first + s)) + (h + (3 if first else 1))
                            wait_apart(pe, st_ready, n, tick) if first else pe.wait_ge(st_ready, n)
                            mm(ps[:, h, 0:NCH // 2], at, states(i, s)[:, c], start=True, stop=True)\
                                .then_inc(z_done, 1)

            scan_steps(0, lambda i, s: st[:, s])
            scan_steps(LCH, lambda i, s: s_from[:, 2 * i + s])
            pe.wait_ge(cmp_step, 3)
            for k in (0, 1):
                ins = mm(ps[0:1, 2 + k, 0:NCH], ones[0:SD, :], sq[:, k], start=True, stop=True)
            ins.then_inc(sums_done, 1)
            pe.wait_ge(flag_ready, 1)
            good = pe.value_load(flag[0:1, 0:1], min_val=0, max_val=1)
            with pe.If(good == 0):
                mm(ps[:, 0, 0:1], at, s_all[:, 0:1], start=True, stop=True).then_inc(seq_z, 1)
                with pe.Fori(1, T) as n:
                    wait_apart(pe, seq_st, n, tick)
                    mm(ps[:, 0, 0:1], at, s_all[:, bass.ds(n, 1)], start=True, stop=True)\
                        .then_inc(seq_z, 1)

            def f_mm(d, slot):
                pe.wait_ge(s_lo, d + 1)
                for t in range(GT):
                    wait(pe, f_added, GT * (d - 2) + (t + 1))
                    b = 4 + 2 * slot + t
                    mm(ps[:, b, :], s1[:, slot, t * P:(t + 1) * P], c1, start=True, stop=False)
                    mm(ps[:, b, :], s2[:, slot, t * P:(t + 1) * P], c2, start=False, stop=True)\
                        .then_inc(f_done, 1)

            pe.wait_ge(c_ready, 1)
            for s in (0, 1):
                f_mm(s, s)
            with pe.Fori(1, X_G // 2) as i:
                for s in (0, 1):
                    f_mm(2 * i + s, s)


def kernel(**inputs):
    import numpy as np
    import concourse.bacc as bacc
    from concourse.bass_utils import run_bass_kernel_spmd

    g = {k.replace("L0_xattn_", ""): np.asarray(a) for k, a in inputs.items()}

    def column(a):
        return a.reshape(FC, P).T

    def padded(a):
        return np.concatenate([a, np.zeros((KPAD - KEYS, a.shape[1]), a.dtype)], axis=0)

    b_q, b_k, b_v = g["b_qkv"].reshape(3, H)
    arrays = {
        "x": g["x"].reshape(T, H),
        "ctx": padded(g["ctx_1024"].reshape(KEYS, H)),
        "ctxb": padded(g["ctxb_2048x64"].reshape(KEYS, SD)).reshape(KT_TILES, P, SD).transpose(1, 0, 2),
        "w_qkv_t": g["W_qkv"].reshape(3, H, FC, P).transpose(3, 0, 2, 1),
        "w_o_t": g["W_o"].reshape(H, FC, P).transpose(2, 1, 0),
        "w_in": g["W_in"].reshape(FC, P, H).transpose(1, 0, 2),
        "bmat": g["Bmat"].reshape(FC, P, SD).transpose(1, 0, 2),
        "w_prog_t": g["W_prog"].T,
        "a_t": g["A"].T,
        "cmat": g["Cmat"],
        "cols": np.stack([column(a) for a in (g["g1"], g["beta1"], g["g2"], g["beta2"], b_q, b_k, g["b_in"])],
                         axis=1),
        "bv_rows": np.broadcast_to(b_v, (P, H)),
        "bo_rows": np.broadcast_to(g["b_o"], (P, H)),
        "b_prog": g["b_prog"].reshape(1, H),
        "k2_rows": np.array([[1.0, 1.0], [0.0, PAD_SCORE]], np.float32),
    }
    arrays = {k: np.ascontiguousarray(a) for k, a in arrays.items()}
    nc = bacc.Bacc("TRN2", target_bir_lowering=False, num_devices=1)
    args = [nc.dram_tensor(k, list(a.shape), mybir.dt.from_np(a.dtype), kind="ExternalInput").ap()
            for k, a in arrays.items()]
    out = nc.dram_tensor("out", [T, H], F32, kind="ExternalOutput").ap()
    build(nc, *args, out)
    r = run_bass_kernel_spmd(nc, [arrays], core_ids=[0])
    return r.results[0]["out"].reshape(1, T, H)
```

```python
from contextlib import ExitStack

import concourse.bass as bass
from concourse import mybir

F32 = mybir.dt.float32
F32R = mybir.dt.float32r
I32 = mybir.dt.int32
ALU = mybir.AluOpType
ACT = mybir.ActivationFunctionType
AX_X = mybir.AxisListType.X

P = 128
T = 4096
KEYS = 3202
KT_TILES = -(-KEYS // P)
KPAD = KT_TILES * P
H = 512
FC = H // P
NH = 8
HD = H // NH
SD = 64
EPS = 1e-5
SCALE = HD ** -0.5

GT = 2
GW = GT * P
CTX_G = KPAD // GW
X_G = T // GW
NG = CTX_G + X_G

QB = 512
QT_N = QB // P
PAIRS = NH // 2
ITERS = (T // QB) * PAIRS
NP = KT_TILES // 2
UNIT_N = 2 * ITERS
MAX_AT = [(0,), (1,), (2,), (3, 4)] + [(s + 1,) for s in range(4, NP - 1)] + [()]
NM = 3 * QT_N + 1
TAIL = 3072
PIECES = [(0, 1024), (1024, 2048), (2048, 3072), (3072, KPAD)]
PAD_SCORE = -2.0 ** 100
PT_SLOTS = 4
PT_SLOT = [0, 1, 2, 3] * 2 + [0, 1, 2] + [0, 1, 2, 3] * 3 + [0, 1, 2]

LCH = 16
NCH = T // LCH
TOL2 = 2.0 ** -38

MOD_LO = 96

LN_STEPS = 14


def wait(eng, sem, value):
    if not (isinstance(value, int) and value <= 0):
        eng.wait_ge(sem, value)


def wait_apart(eng, sem, value, tick):
    wait(eng, sem, value)
    if not isinstance(value, int):
        eng.sem_inc(tick, 1)


def pt_slot(w2, s):
    return PT_SLOT[NP * w2 + s]


def pt_user_before(w, w2, s):
    i = NP * w2 + s
    j = max(k for k in range(i - 2 * NP, i) if PT_SLOT[k % (2 * NP)] == PT_SLOT[i])
    return w - w2 + j // NP, j % NP


def pe_sum_index(s):
    return max(s // 2 - 1, 0)


SUMS_V = NP // 2 + 1
SUMS_G = NP // 2 + 1


def build(nc, x, ctx, ctxb, w_qkv_t, w_o_t, w_in, bmat, w_prog_t, a_t, cmat, cols, bv_rows, bo_rows,
          b_prog, k2_rows, out):
    es = ExitStack()
    with es:
        def sb(name, shape, dt=F32):
            return es.enter_context(nc.sbuf_tensor(name, shape, dt))

        def sem(name):
            return es.enter_context(nc.semaphore(name))

        q_scratch = nc.dram_tensor("q_scratch", [ITERS, P, QB], F32).ap()
        o_scratch = nc.dram_tensor("o_scratch", [ITERS, 2, P, QT_N * HD], F32).ap()

        kt = sb("kt", [P, FC * KPAD])
        big = sb("big", [P, KT_TILES * H + 3 * FC * H])
        k1 = sb("k1", [P, 2, KPAD], F32R)
        k2 = sb("k2", [P, KPAD], F32R)
        q_max = sb("q_max", [P, QB], F32R)
        q1 = sb("q1", [P, 2, QB], F32R)
        q2 = sb("q2", [P, 2, QB], F32R)
        work = sb("work", [P, 4096])
        wo_qo = sb("wo_qo", [P, FC, H])
        qt_sb = sb("qt_sb", [P, QB])[:, :]
        k2_cols = sb("k2_cols", [HD + 2, 2])
        w_u = sb("w_u", [P, FC, SD])
        ident = sb("ident", [P, P])
        fold = sb("fold", [P, HD])
        ones = sb("ones", [P, 1])
        col = sb("col", [P, 7, FC])
        c_aug = sb("c_aug", [SD + 1, H])
        cu = sb("cu", [SD, 1])
        mean = sb("mean", [SD, 1])
        stats = sb("stats", [P, GT, 6])
        mv = sb("mv", [P, GT, 2])
        ve = sb("ve", [P, GT])
        yi = sb("yi", [P, GT], I32)
        ya = sb("ya", [P, GT])
        yb = sb("yb", [P, GT])
        mx_part = sb("mx_part", [P, QT_N, 4])
        mx_first = sb("mx_first", [P, QT_N, 7])
        mx = sb("mx", [P, QT_N])
        rden = sb("rden", [P, QT_N])
        flag_f = sb("flag_f", [1, 2])
        flag = sb("flag", [1, 1], I32)
        ps = es.enter_context(nc.psum_tensor("ps", [P, 8, 512], F32))

        g1, be1, g2, be2, bq, bk, bin_ = (col[:, i, :] for i in range(7))
        kt4 = kt[:, :].rearrange("p (c k) -> p c k", c=FC)
        v = big[:, 0:KT_TILES * H].rearrange("p (t f) -> p t f", t=KT_TILES)
        pt = big[:, KT_TILES * H:KT_TILES * H + PT_SLOTS * 2 * QB].rearrange("p (s k) -> p s k", s=PT_SLOTS)
        sums = big[:, KT_TILES * H + PT_SLOTS * 2 * QB:].rearrange("p (e k) -> p e k", e=2)
        bv = wo_qo[:, 3, :]
        at = wo_qo[0:SD, 3, 0:2 * SD]
        qt_first = wo_qo[:, 0, :]
        o_half = wo_qo[:, 1, :]
        o_out = wo_qo[:, 2, :].rearrange("p (h q d) -> p h q d", h=2, q=QT_N)
        w3 = big[:, KT_TILES * H:KT_TILES * H + 3 * FC * H].rearrange("p (w c n) -> p w c n", w=3, c=FC)
        win_sb = v[:, 22:26, :]
        b_sb = v[:, 21, 0:FC * SD].rearrange("p (c s) -> p c s", c=FC)
        cb_sb = big[:, 17 * H:17 * H + KT_TILES * SD].rearrange("p (t s) -> p t s", t=KT_TILES)
        wp_sb = v[0:SD, 16, :]
        bp = v[0:1, 15, :]
        cb_sum = v[:, 14, 0:SD]
        xs = work[:, 0:2048].rearrange("p (s t f) -> p s t f", s=2, t=GT)
        xn = work[:, 1024:2048].rearrange("p (t f) -> p t f", t=GT)
        nt = work[:, 2048:4096].rearrange("p (s c k) -> p s c k", s=2, c=FC)
        v_head = work[:, 0:2 * KT_TILES * HD].rearrange("p (s t d) -> p s t d", s=2, t=KT_TILES)
        k1_flat = k1[:, :, :].rearrange("p s k -> p (s k)")

        def w_part(w, lo):
            flat = k2[:, 0:FC * H] if (w, lo) == (1, 1) else k1_flat[:, (2 - w + 2 * lo) * FC * H:(3 - w + 2 * lo) * FC * H]
            return flat.rearrange("p (c n) -> p c n", c=FC)

        def n_part(slot, lo, c):
            a = (k2[:, FC * H:FC * H + 2 * H], q1[:, :, :].rearrange("p s k -> p (s k)"),
                 q2[:, :, :].rearrange("p s k -> p (s k)"))
            if slot and lo:
                return k1_flat[:, 12 * H + c * GW:12 * H + (c + 1) * GW] if c < 2 \
                    else q_max[:, (c - 2) * GW:(c - 1) * GW]
            return a[slot + 2 * lo][:, c * GW:(c + 1) * GW]

        s_all = kt[0:SD, 0:T + 1]
        u_all = kt[SD:2 * SD, 0:T]
        a = T + 4
        og = kt[:, a:a + 2048].rearrange("p (s t h d) -> p s t h d", s=2, t=GT, h=NH)
        w_o = kt[:, a + 2048:a + 4096].rearrange("p (c n) -> p c n", c=FC)
        ot = kt[:, a + 4096:a + 6144].rearrange("p (s c k) -> p s c k", s=2, c=FC)
        xb = kt[:, a + 6144:a + 8192].rearrange("p (s t f) -> p s t f", s=2, t=GT)
        bo = kt[:, a + 8192:a + 8192 + H]
        x1 = big[:, 0:(T // P) * H].rearrange("p (t f) -> p t f", t=T // P)
        st = work[0:SD, 0:2 * NCH].rearrange("p (s c) -> p s c", s=2)
        sg = work[SD:2 * SD, 0:NCH]
        end1 = work[0:SD, 1024:1024 + NCH]
        diff = work[0:SD, 1280:1280 + NCH]
        sq = work[0:SD, 1536:1536 + 2 * NCH].rearrange("p (s c) -> p s c", s=2)
        lhs_row = work[0:1, 2048:2048 + NCH]
        ok_row = work[0:1, 2304:2304 + NCH]
        e_row = work[0:1, 2560:2560 + NCH]
        u_steps = u_all.rearrange("p (c k) -> p k c", k=LCH)
        s_from = s_all[:, 0:T].rearrange("p (c k) -> p k c", k=LCH)
        s_to = s_all[:, 1:T + 1].rearrange("p (c k) -> p k c", k=LCH)
        c1 = k1[:, 0, 0:H]
        c2 = k2[0:MOD_LO + 1, 0:H]
        s1 = k1[:, 1, 0:2 * GW].rearrange("p (s k) -> p s k", s=2)
        s2 = k2[0:MOD_LO + 1, H:H + 2 * GW].rearrange("p (s k) -> p s k", s=2)

        wo_hi = k1_flat[:, H:H + FC * H].rearrange("p (c n) -> p c n", c=FC)
        wo_lo = (k1_flat[:, 5 * H:6 * H], q_max[:, :], q1[:, 0, :], q2[:, 0, :])

        def o_part(slot, lo, c):
            a = k1_flat[:, KPAD + H + slot * 2 * H:] if lo else k2[:, 2 * H + slot * 2 * H:]
            return a[:, c * GW:(c + 1) * GW]

        setup_loaded = sem("setup_loaded"); w_loaded = [sem("wq_loaded"), sem("wk_loaded"), sem("wv_loaded")]; cols_loaded = sem("cols_loaded")
        cb_summed = sem("cb_summed"); wo_loaded = sem("wo_loaded")
        consts = sem("consts"); setup_mm = sem("setup_mm"); setup_ev = sem("setup_ev")
        ln_step = sem("ln_step")
        tick = sem("tick")
        xs_loaded = [sem("xs_loaded_0"), sem("xs_loaded_1")]; normed = sem("normed"); transposed = sem("transposed")
        w_hi = sem("w_hi"); w_lo = sem("w_lo"); n_lo = sem("n_lo")
        nt_ready = sem("nt_ready"); kq_done = sem("kq_done"); kq_evac = sem("kq_evac")
        v_done = sem("v_done"); v_evac = sem("v_evac"); q_stored = [sem("q_stored_0"), sem("q_stored_1")]
        qt_loaded = sem("qt_loaded"); wo_hi_ready = sem("wo_hi_ready"); wo_lo_ready = sem("wo_lo_ready"); ot_lo_ready = sem("ot_lo_ready")
        bo_loaded = sem("bo_loaded"); at_loaded = sem("at_loaded")
        q2_ones_set = sem("q2_ones_set"); k2_rows_set = sem("k2_rows_set")
        k_hi = sem("k_hi"); k_lo = sem("k_lo"); k2_ready = sem("k2_ready")
        qm_ready = sem("qm_ready"); q1_ready = sem("q1_ready"); q2_ready = sem("q2_ready")
        v_even_loaded = sem("v_even_loaded"); v_odd_loaded = sem("v_odd_loaded")
        max_done = sem("max_done"); max_taken = sem("max_taken"); first_free = sem("first_free"); max_ready = sem("max_ready")
        max_turned = sem("max_turned"); shift_ready = sem("shift_ready")
        scored = sem("scored"); exped = sem("exped"); pv_done = sem("pv_done")
        summed_v = sem("summed_v"); summed_g = sem("summed_g"); half_ready = sem("half_ready")
        folded = sem("folded"); rden_ready = sem("rden_ready"); o_scaled = sem("o_scaled")
        o_even_free = sem("o_even_free"); o_odd_free = sem("o_odd_free")
        og_loaded = [sem("og_loaded_0"), sem("og_loaded_1")]; x2_loaded = [sem("x2_loaded_0"), sem("x2_loaded_1")]; xb_ready = sem("xb_ready")
        o_turned = sem("o_turned"); ot_ready = sem("ot_ready"); y_done = sem("y_done")
        x1_ready = sem("x1_ready"); normed2 = sem("normed2"); n2_turned = sem("n2_turned")
        n2t_ready = sem("n2t_ready"); u_done = sem("u_done"); u_ready = sem("u_ready")
        z_done = sem("z_done"); silu_done = sem("silu_done"); st_ready = sem("st_ready")
        cmp_step = sem("cmp_step"); sums_done = sem("sums_done")
        flag_ready = sem("flag_ready")
        seq_z = sem("seq_z"); seq_silu = sem("seq_silu"); seq_st = sem("seq_st")
        c_cleared = sem("c_cleared"); c_hi = sem("c_hi"); c_ready = sem("c_ready"); s_hi = sem("s_hi"); s_lo = sem("s_lo"); f_done = sem("f_done"); f_added = sem("f_added"); stored = sem("stored")

        block = es.enter_context(nc.Block())

        def b_steps(eng, front, back, after=lambda g: None,
                    before=lambda i, s: None, inside=lambda i, s: None):
            front(0, 0, 1, True)
            for g in (0, 1):
                front(g + 1, (g + 1) % 2, (g + 1) // 2 + 1, True)
                back(g, g % 2)
            with eng.Fori(0, 5) as i:
                for s in (0, 1):
                    front(2 * i + (3 + s), (1 + s) % 2, i + (2 + s), True)
                    back(2 * i + (2 + s), s)
            for g in (12, 13, 14):
                front(g + 1, (g + 1) % 2, (g + 1) // 2 + 1, False)
                back(g, g % 2)
                after(g)
            with eng.Fori(0, 6) as i:
                for s in (0, 1):
                    before(i, s)
                    front(2 * i + (16 + s), s, i + 9, False)
                    inside(i, s)
                    back(2 * i + (15 + s), 1 - s, i + 1, s)
            front(NG - 1, (NG - 1) % 2, (NG - 1) // 2 + 1, False)
            back(NG - 2, (NG - 2) % 2)
            after(NG - 2)
            back(NG - 1, (NG - 1) % 2)
            after(NG - 1)

        def x_group(g, block_half):
            return block_half or ((g - CTX_G) // 2, (g - CTX_G) % 2)

        def d_steps(eng, turn, project, turn2, finish):
            def step(d, slot, more=True, first=False):
                if more:
                    turn(d + 2, slot)
                project(d + 1, 1 - slot, 0)
                if not first:
                    finish(d - 1, 1 - slot)
                project(d + 1, 1 - slot, 1)
                turn2(d, slot)

            turn(0, 0)
            turn(1, 1)
            for t in range(GT):
                project(0, 0, t)
            for d in (0, 1):
                step(d, d, first=(d == 0))
            with eng.Fori(0, 6) as i:
                for s in (0, 1):
                    step(2 * i + (2 + s), s)
            step(X_G - 2, 0, False)
            turn2(X_G - 1, 1)
            finish(X_G - 2, 0)
            finish(X_G - 1, 1)

        def scan_halves():
            return ((h, slice(h * NCH // 2, (h + 1) * NCH // 2)) for h in (0, 1))

        def c_steps(eng, unit):
            for hh in (0, 1):
                unit(0, hh, True, False)
            with eng.Fori(1, ITERS - 1) as it:
                for hh in (0, 1):
                    unit(it, hh, False, False)
            for hh in (0, 1):
                unit(ITERS - 1, hh, False, True)

        def ahead(it, hh, n):
            k = hh + n
            return 2 * it + k, it + k // 2, k % 2

        @block.sync
        def _(sp):
            def load_ctx(g, slot):
                wait(sp, transposed, 2 * (g - 1))
                sp.dma_start(xs[:, slot], ctx.rearrange("(g t p) f -> g p t f", p=P, t=GT)[g])\
                    .then_inc(xs_loaded[slot], 16)

            def load_x(h, slot):
                wait(sp, transposed, 2 * (h + CTX_G - 1))
                sp.dma_start(xs[:, slot], x.rearrange("(g t p) f -> g p t f", p=P, t=GT)[h])\
                    .then_inc(xs_loaded[slot], 16)

            def store_q(h, blk, half):
                wait(sp, kq_evac, FC * (h + CTX_G + 1))
                dst = q_scratch.rearrange("(b c) p k -> b p c k", c=FC)[blk]
                sp.dma_start(dst[:, :, half * GW:(half + 1) * GW],
                             wo_qo[:, :, half * GW:(half + 1) * GW]).then_inc(q_stored[half], 16)

            def v_copy(w, it, hh):
                wait(sp, pv_done, NP * (w - 1))
                vv = v.rearrange("p t (c s d) -> p c s t d", c=FC, s=2)
                sp.dma_start(v_head[:, hh], vv[:, it % PAIRS, hh]).then_inc((v_even_loaded, v_odd_loaded)[hh], 16)

            load_ctx(0, 0)
            sp.dma_start(col[:, :, :], cols).then_inc(cols_loaded, 16)
            load_ctx(1, 1)
            for dst, src in ((b_sb, bmat), (win_sb, w_in), (cb_sb, ctxb), (wp_sb, w_prog_t),
                             (bp, b_prog),
                             (c_aug[0:SD, :], cmat), (bv, bv_rows),
                             (k2_cols[HD:HD + 2, :], k2_rows)):
                sp.dma_start(dst, src).then_inc(setup_loaded, 16)
            for w in (2, 1, 0):
                sp.dma_start(w3[:, w], w_qkv_t[:, w]).then_inc(w_loaded[w], 16)
            with sp.Fori(1, CTX_G // 2) as i:
                for s in (0, 1):
                    load_ctx(2 * i + s, s)
            load_ctx(CTX_G - 1, 0)
            for h in (0, 1, 2):
                load_x(h, (CTX_G + h) % 2)
            for s in (0, 1):
                load_x(3 + s, s)
                store_q(s, 0, s)
            for half in (0, 1):
                sp.wait_ge(q_stored[half], 16)
            sp.dma_start(qt_sb, q_scratch[0]).then_inc(qt_loaded, 16)
            with sp.Fori(1, X_G // 2 - 2) as i:
                for s in (0, 1):
                    load_x(2 * i + (3 + s), s)
                    store_q(2 * i + s, i, s)
            load_x(X_G - 1, 0)
            for h in range(X_G - 4, X_G - 1):
                store_q(h, h // 2, h % 2)
            sp.wait_ge(transposed, 2 * NG)
            v_copy(0, 0, 0)
            store_q(X_G - 1, X_G // 2 - 1, 1)
            for half in (0, 1):
                sp.wait_ge(q_stored[half], 16 * (X_G // 2))
            for half in (0, 1):
                sp.dma_start(at[:, half * SD:(half + 1) * SD], a_t).then_inc(at_loaded, 16)

            def store_o(it, hh):
                dst = o_scratch[it, hh]
                sp.wait_ge(o_scaled, 2 * it + hh + 1)
                sp.dma_start(dst, o_out[:, hh, :, :].rearrange("p q d -> p (q d)"))\
                    .then_inc((o_even_free, o_odd_free)[hh], 16)

            def c_unit(it, hh, first, last):
                if not (last and hh == 1):
                    v_copy(*ahead(it, hh, 1))
                if hh == 0:
                    if not first:
                        store_o(it - 1, 1)
                    if not last:
                        sp.wait_ge(q2_ready, 2 * it + 2)
                        sp.dma_start(qt_sb, q_scratch[it + 1]).then_inc(qt_loaded, 16)
                else:
                    store_o(it, 0)

            def load_og(half, blk):
                src = o_scratch.rearrange("(b c) h p k -> b p (c h) k", c=FC)[blk]
                for t in range(GT):
                    q = half * GT + t
                    sp.dma_start(og[:, half, t], src[:, :, q * HD:(q + 1) * HD]).then_inc(og_loaded[half], 16)

            def load_x2(d, half):
                sp.dma_start(xb[:, half], x.rearrange("(g t p) f -> g p t f", p=P, t=GT)[d])\
                    .then_inc(x2_loaded[half], 16)

            c_steps(sp, c_unit)
            sp.wait_ge(k_lo, 4 * UNIT_N)
            sp.wait_ge(k2_ready, 4 * UNIT_N)
            sp.dma_start(w_o, w_o_t).then_inc(wo_loaded, 16)
            sp.dma_start(bo, bo_rows).then_inc(bo_loaded, 16)
            sp.wait_ge(o_odd_free, 16 * ITERS)
            for half in (0, 1):
                load_og(half, 0)
                load_x2(half, half)
            store_o(ITERS - 1, 1)
            sp.wait_ge(o_even_free, 16 * (ITERS + 1))
            sp.wait_ge(o_odd_free, 16 * (ITERS + 1))

            with sp.Fori(1, X_G // 2) as i:
                for half in (0, 1):
                    d = 2 * i + half
                    sp.wait_ge(o_turned, 2 * (d - 1))
                    load_og(half, i)
                    sp.wait_ge(x1_ready, GT * (d - 1))
                    load_x2(d, half)

            def f_store(d):
                sp.wait_ge(f_added, GT * (d + 1))
                sp.dma_start(out.rearrange("(g t p) f -> g p t f", p=P, t=GT)[d],
                             x1[:, bass.ds(GT * d, GT), :]).then_inc(stored, 16)

            with sp.Fori(0, X_G) as d:
                f_store(d)
            sp.wait_ge(stored, 16 * X_G)

        @block.gpsimd
        def _(pool):
            nc.gpsimd.memset(ident[:, :], 0.0).then_inc(consts, 1)
            nc.gpsimd.memset(fold[:, :], 0.0).then_inc(consts, 1)
            nc.gpsimd.memset(ones[:, :], 1.0).then_inc(consts, 1)
            pool.wait_ge(consts, 3)
            nc.gpsimd.affine_select(out=ident[:, :], in_=ident[:, :], compare_op=ALU.not_equal, fill=1.0,
                                    base=0, pattern=[[-1, P]], channel_multiplier=1).then_inc(consts, 1)
            nc.gpsimd.affine_select(out=fold[:, :], in_=fold[:, :], compare_op=ALU.not_equal, fill=1.0,
                                    base=0, pattern=[[-1, HD]], channel_multiplier=1).then_inc(consts, 1)
            pool.wait_ge(consts, 5)
            nc.gpsimd.affine_select(out=fold[:, :], in_=fold[:, :], compare_op=ALU.not_equal, fill=1.0,
                                    base=-HD, pattern=[[-1, HD]], channel_multiplier=1).then_inc(consts, 1)

            def w_low(w):
                pool.wait_ge(w_hi, 3 - w)
                nc.gpsimd.tensor_tensor(w_part(w, 1), w3[:, w], w_part(w, 0).bitcast(F32), ALU.subtract)\
                    .then_inc(w_lo, 1)

            def n_low(g, slot):
                for c in range(FC):
                    pool.wait_ge(nt_ready, FC * g + (c + 1))
                    nc.gpsimd.tensor_tensor(n_part(slot, 1, c), nt[:, slot, c], n_part(slot, 0, c).bitcast(F32),
                                            ALU.subtract).then_inc(n_lo, 1)

            w_low(2)
            n_low(0, 0)
            w_low(1)
            n_low(1, 1)
            with pool.Fori(1, CTX_G // 2) as i:
                for s in (0, 1):
                    n_low(2 * i + s, s)
            n_low(CTX_G - 1, 0)
            pool.wait_ge(n_lo, FC * CTX_G)

            def k_low(v, v_it, hh, p, own_sums):
                a, b = slice(HD * hh, HD * hh + HD), slice(HD * (1 - hh), HD * (1 - hh) + HD)
                c = slice(*PIECES[p])
                wait(pool, summed_g, own_sums)
                pool.wait_ge(k_hi, 4 * v + (p + 1))
                nc.gpsimd.tensor_tensor(k1[b, hh, c], kt4[a, v_it % PAIRS, c], k1[a, hh, c].bitcast(F32),
                                        ALU.subtract).then_inc(k_lo, 1)
                pool.wait_ge(k_lo, 4 * v + (p + 1))

            def fold_halves(w):
                pool.wait_ge(summed_g, SUMS_G * w + (SUMS_G - 2))
                nc.gpsimd.tensor_tensor(sums[:, 1, 0:QB], sums[:, 1, 0:QB], sums[:, 1, QB:], ALU.add)\
                    .then_inc(summed_g, 1)

            def take_sums(w):
                pool.wait_ge(summed_v, SUMS_V * (w + 1))
                pool.wait_ge(summed_g, SUMS_G * w + (SUMS_G - 1))
                nc.gpsimd.tensor_tensor(sums[:, 1, 0:QB], sums[:, 1, 0:QB], sums[:, 0, 0:QB], ALU.add)\
                    .then_inc(summed_g, 1)

            for p in range(4):
                k_low(0, 0, 0, p, 0)
            pool.wait_ge(q1_ready, 1)
            nc.gpsimd.tensor_tensor(q2[0:HD, 0, :], qt_first[0:HD], q1[0:HD, 0, :].bitcast(F32), ALU.subtract)\
                .then_inc(q2_ready, 1)
            pool.wait_ge(q2_ready, 1)
            for p in range(2):
                k_low(1, 0, 1, p, 0)

            def c_unit(it, hh, first, last):
                w = 2 * it + hh
                w1, it1, hh1 = ahead(it, hh, 1)
                w2, it2, hh2 = ahead(it, hh, 2)
                if not (first and hh == 0):
                    take_sums(w - 1)
                for s in range(3, NP, 2):
                    pool.wait_ge(exped, NP * w + (s + 1))
                    if s == 3:
                        wait(pool, folded, w)
                        a = pt[:, pt_slot(hh, 1)]
                    else:
                        pool.wait_ge(summed_g, SUMS_G * w + pe_sum_index(s))
                        a = sums[:, 1]
                    nc.gpsimd.tensor_tensor(sums[:, 1], a, pt[:, pt_slot(hh, s)], ALU.add).then_inc(summed_g, 1)
                    if s == 3 and not (last and hh == 1):
                        for p in (2, 3):
                            k_low(w1, it1, hh1, p, SUMS_G * w + 1)
                    if s in (5, 9) and not last:
                        k_low(w2, it2, hh2, (s - 5) // 4, SUMS_G * w + (pe_sum_index(s) + 1))
                fold_halves(w)

            c_steps(pool, c_unit)
            take_sums(UNIT_N - 1)
            pool.wait_ge(bo_loaded, 16)

            def add_bias(d, slot):
                pool.wait_ge(x2_loaded[slot], 8 * (d - slot) + 16)
                for t in range(GT):
                    ins = nc.gpsimd.tensor_tensor(xb[:, slot, t], xb[:, slot, t], bo, ALU.add)
                ins.then_inc(xb_ready, 1)

            def turn(d, slot):
                for k in range(2):
                    pool.wait_ge(ot_ready, 2 * d + (k + 1))
                    for c in (2 * k, 2 * k + 1):
                        ins = nc.gpsimd.tensor_tensor(o_part(slot, 1, c), ot[:, slot, c],
                                                      o_part(slot, 0, c).bitcast(F32), ALU.subtract)
                    ins.then_inc(ot_lo_ready, 1)
                if not (isinstance(d, int) and d < 2):
                    add_bias(d, slot)

            for slot in (0, 1):
                add_bias(slot, slot)
            nothing = lambda *_: None
            d_steps(pool, turn, nothing, nothing, nothing)

            pool.wait_ge(xb_ready, X_G)
            with pool.Fori(0, X_G // 2) as i:
                for s in (0, 1):
                    d = 2 * i + s
                    pool.wait_ge(s_hi, d + 1)
                    nc.gpsimd.tensor_tensor(s1[SD:2 * SD, s], s_all[:, bass.ds(d * GW + 1, GW)],
                                            s1[0:SD, s].bitcast(F32), ALU.subtract).then_inc(s_lo, 1)

        @block.scalar
        def _(act):
            def b_front(g, slot, loads, is_ctx):
                wait(act, kq_done, FC * (g - 1))
                for c in range(FC):
                    if c % 2 == 0:
                        act.wait_ge(transposed, 2 * g + (c // 2 + 1))
                    for dst in (nt[:, slot, c], n_part(slot, 0, c)) if is_ctx else (nt[:, slot, c],):
                        ins = nc.scalar.activation(dst, ps[:, c // 2, (c % 2) * GW:(c % 2 + 1) * GW],
                                                   ACT.Identity, bias=be1[:, c:c + 1], scale=g1[:, c:c + 1])
                    ins.then_inc(nt_ready, 1)
                if isinstance(g, int) and g == 0:
                    for w in (2, 1):
                        act.wait_ge(w_loaded[w], 16)
                        nc.scalar.activation(w_part(w, 0), w3[:, w], ACT.Copy).then_inc(w_hi, 1)

            def b_back(g, slot, *block_half):
                is_ctx = isinstance(g, int) and g < CTX_G or not isinstance(g, int) and not block_half
                if not is_ctx:
                    if isinstance(g, int) and g == CTX_G:
                        act.wait_ge(v_evac, GT * CTX_G)
                    blk, half = x_group(g, block_half)
                    wait(act, q_stored[half], 16 * blk)
                for c in range(FC):
                    act.wait_ge(kq_done, FC * g + (c + 1))
                    if is_ctx:
                        dst = kt4[:, c, bass.ds(g * GW, GW)]
                    else:
                        dst = wo_qo[:, c, half * GW:(half + 1) * GW]
                    nc.scalar.activation(dst, ps[:, 2 + c, 0:GW], ACT.Identity,
                                         bias=(bk if is_ctx else bq)[:, c:c + 1]).then_inc(kq_evac, 1)

            act.wait_ge(cols_loaded, 16)
            def own(hh):
                return slice(HD * hh, HD * hh + HD), slice(HD * (1 - hh), HD * (1 - hh) + HD)

            def k_high(v_it, hh, p):
                a, _ = own(hh)
                c = slice(*PIECES[p])
                nc.scalar.activation(k1[a, hh, c], kt4[a, v_it % PAIRS, c], ACT.Copy).then_inc(k_hi, 1)

            def k2_high(v_it, hh, p):
                a, _ = own(hh)
                c = slice(*PIECES[p])
                nc.scalar.activation(k2[0:HD, c], kt4[a, v_it % PAIRS, c], ACT.Copy).then_inc(k2_ready, 1)

            def q_high(dst, hh, done, src=qt_sb):
                a, b = own(hh)
                nc.scalar.activation(dst[a], src[a, :], ACT.Copy)
                nc.scalar.activation(dst[b], src[a, :], ACT.Copy).then_inc(done, 1)

            def shift(v, slot):
                act.wait_ge(max_turned, v + 1)
                nc.scalar.activation(q2[HD:HD + 1, slot, :], ps[0:1, 7, :], ACT.Copy, scale=-1.0)\
                    .then_inc(shift_ready, 1)

            def c_first(g):
                if g == CTX_G:
                    act.wait_ge(kq_evac, FC * (CTX_G + 1))
                    for p in range(4):
                        k_high(0, 0, p)
                if g == CTX_G + 1:
                    act.wait_ge(kq_evac, FC * (CTX_G + 2))
                    act.wait_ge(q2_ones_set, 1)
                    q_high(q_max[:, :], 0, qm_ready, qt_first)
                    q_high(q1[:, 0], 0, q1_ready, qt_first)
                    for p in range(2):
                        k_high(0, 1, p)
                    act.wait_ge(q2_ready, 1)
                if g == NG - 2:
                    for c, cols_c in ((0, slice(0, KEYS)), (1, slice(KEYS, KPAD))):
                        n = cols_c.stop - cols_c.start
                        ins = nc.scalar.activation(k2[HD:HD + 2, cols_c], k2_cols[HD:HD + 2, c:c + 1].to_broadcast([2, n]),
                                                   ACT.Copy)
                    ins.then_inc(k2_rows_set, 1)
                    for p in range(2):
                        k2_high(0, 0, p)
                    act.wait_ge(max_done, NM)
                    act.wait_ge(qt_loaded, 16)
                    q_high(q_max[:, :], 1, qm_ready)
                if g == NG - 1:
                    shift(0, 0)

            b_steps(act, b_front, b_back, c_first)

            def take_half(w):
                act.wait_ge(pv_done, NP * (w + 1))
                wait(act, folded, w)
                nc.scalar.activation(o_half[:, :], ps[:, 6, :], ACT.Copy).then_inc(half_ready, 1)

            def exp_pair(it, hh, s, first):
                w = 2 * it + hh
                act.wait_ge(scored, NP * w + (s + 1))
                if not (first and NP * hh + s < PT_SLOTS):
                    w_b, s_b = pt_user_before(w, hh, s)
                    act.wait_ge(pv_done, NP * w_b + (s_b + 1))
                    if s_b % 2:
                        act.wait_ge(summed_g, SUMS_G * w_b + (pe_sum_index(s_b) + 1))
                    else:
                        act.wait_ge(summed_v, SUMS_V * w_b + (pe_sum_index(s_b) + 1))
                b = 2 * ((NP * hh + s) % 2)
                nc.scalar.activation(pt[:, pt_slot(hh, s)], ps[:, b:b + 2, :].rearrange("p a b -> p (a b)"),
                                     ACT.Exp, scale=SCALE).then_inc(exped, 1)

            def c_unit(it, hh, first, last):
                w = 2 * it + hh
                w1, it1, hh1 = ahead(it, hh, 1)
                w2, it2, hh2 = ahead(it, hh, 2)
                next1 = not (last and hh == 1)
                next2 = not last
                for s in range(NP):
                    if s == NP - 1 and next1:
                        shift(w1, hh1)
                    exp_pair(it, hh, s, first)
                    if s == 0:
                        if not (first and hh == 0):
                            take_half(w - 1)
                    if s == 1 and next1:
                        act.wait_ge(qt_loaded, 16 * (it1 + 1))
                        q_high(q1[:, hh1], hh1, q1_ready)
                    if s in (2, 4) and next1:
                        k_high(it1, hh1, 2 if s == 2 else 3)
                    if s == 3:
                        for p in (2, 3):
                            k2_high(it, hh, p)
                    for p, (s_k, s_k2) in enumerate(((5, 6), (9, 10))):
                        if s == s_k and next2:
                            k_high(it2, hh2, p)
                        if s == s_k2 and next1:
                            k2_high(it1, hh1, p)
                    if s in (9, 10) and last and hh == 1:
                        act.wait_ge(wo_loaded, 16)
                        c = slice(2 * (s - 9), 2 * (s - 9) + 2)
                        nc.scalar.activation(wo_hi[:, c], w_o[:, c], ACT.Copy).then_inc(wo_hi_ready, 1)
                    if s == 11 and next2:
                        act.wait_ge(max_done, NM * (w1 + 1))
                        act.wait_ge(qt_loaded, 16 * (it2 + 1))
                        q_high(q_max[:, :], hh2, qm_ready)

            c_steps(act, c_unit)
            take_half(UNIT_N - 1)

            def turn(d, slot):
                wait(act, y_done, GT * (d - 1))
                for k in range(2):
                    act.wait_ge(o_turned, 2 * d + (k + 1))
                    nc.scalar.activation(ot[:, slot, 2 * k:2 * k + 2].rearrange("p c k -> p (c k)"),
                                         ps[:, k, :], ACT.Copy)
                    for c in (2 * k, 2 * k + 1):
                        ins = nc.scalar.activation(o_part(slot, 0, c), ps[:, k, (c % 2) * GW:(c % 2 + 1) * GW],
                                                   ACT.Copy)
                    ins.then_inc(ot_ready, 1)

            def turn2(d, slot):
                wait(act, u_done, d - 1)
                for c in range(FC):
                    if c % 2 == 0:
                        act.wait_ge(n2_turned, 2 * d + (c // 2 + 1))
                    nc.scalar.activation(nt[:, slot, c], ps[:, 4 + c // 2, (c % 2) * GW:(c % 2 + 1) * GW],
                                         ACT.Identity, bias=be2[:, c:c + 1], scale=g2[:, c:c + 1])\
                        .then_inc(n2t_ready, 1)

            def finish(d, slot):
                act.wait_ge(u_done, d + 1)
                nc.scalar.activation(u_all[:, bass.ds(d * GW, GW)], ps[0:SD, 6, 0:GW], ACT.Identity,
                                     bias=cu[:, 0:1]).then_inc(u_ready, 1)

            d_steps(act, turn, lambda d, slot, t: None, turn2, finish)
            act.wait_ge(c_cleared, 1)
            for rows in (slice(0, SD), slice(SD, 2 * SD)):
                nc.scalar.activation(c1[rows], c_aug[0:SD, :], ACT.Copy)
            nc.scalar.activation(c2[SD:SD + 1], c_aug[SD:SD + 1, :], ACT.Copy).then_inc(c_hi, 1)

            def scan_steps(first):
                with act.Fori(0, LCH // 2) as i:
                    for s in (0, 1):
                        for h, c in scan_halves():
                            act.wait_ge(z_done, 2 * (2 * i + (first + s)) + (h + 1))
                            nc.scalar.activation(sg[:, c], ps[SD:2 * SD, h, 0:NCH // 2], ACT.Silu)\
                                .then_inc(silu_done, 1)

            scan_steps(0)
            scan_steps(LCH)
            act.wait_ge(flag_ready, 1)
            good = act.value_load(flag[0:1, 0:1], min_val=0, max_val=1)
            with act.If(good == 0):
                with act.Fori(0, T) as n:
                    act.wait_ge(seq_z, n + 1)
                    nc.scalar.activation(sg[:, 0:1], ps[SD:2 * SD, 0, 0:1], ACT.Silu).then_inc(seq_silu, 1)
                act.wait_ge(seq_st, T)

            def f_high(d, slot):
                wait(act, f_done, GT * (d - 1))
                src = s_all[:, bass.ds(d * GW + 1, GW)]
                nc.scalar.activation(s1[0:SD, slot], src, ACT.Copy)
                nc.scalar.activation(s2[0:SD, slot], src, ACT.Copy).then_inc(s_hi, 1)

            for s in (0, 1):
                f_high(s, s)
            with act.Fori(1, X_G // 2) as i:
                for s in (0, 1):
                    f_high(2 * i + s, s)

        @block.vector
        def _(dve):
            def layernorm(n, src, dst, dst_free, done):
                step = [LN_STEPS * n, 0]

                def link(ins):
                    step[1] += 1
                    ins.then_inc(ln_step, 1)
                    wait_apart(dve, ln_step, step[0] + step[1], tick)

                for t in range(GT):
                    ins = nc.vector.bn_stats(stats[:, t, :], src(t))
                link(ins)
                for t in range(GT):
                    ins = nc.vector.bn_aggr(mv[:, t, :], stats[:, t, :])
                link(ins)
                link(nc.vector.tensor_scalar(ve[:, :], mv[:, :, 1], EPS, None, ALU.add))
                link(nc.vector.tensor_scalar(yi[:, :], ve[:, :].bitcast(I32), 1, None,
                                             ALU.logical_shift_right))
                link(nc.vector.tensor_scalar(ya[:, :].bitcast(I32), yi[:, :], -1, 0x5F3759DF,
                                             ALU.mult, ALU.add))
                for _ in range(3):
                    link(nc.vector.tensor_tensor(yb[:, :], ya[:, :], ya[:, :], ALU.mult))
                    link(nc.vector.scalar_tensor_tensor(out=yb[:, :], in0=yb[:, :], scalar=-0.5,
                                                        in1=ve[:, :], op0=ALU.mult, op1=ALU.mult))
                    link(nc.vector.scalar_tensor_tensor(out=ya[:, :], in0=yb[:, :], scalar=1.5,
                                                        in1=ya[:, :], op0=ALU.add, op1=ALU.mult))
                assert step[1] == LN_STEPS
                dst_free()
                for t in range(GT):
                    ins = nc.vector.tensor_scalar(dst(t), src(t), mv[:, t, 0:1], ya[:, t:t + 1],
                                                  ALU.subtract, ALU.mult)
                ins.then_inc(done, 1)

            def setup():
                dve.wait_ge(setup_loaded, 16 * 8)
                nc.vector.tensor_reduce(cb_sum, cb_sb.rearrange("p t s -> p s t"), AX_X, ALU.add)\
                    .then_inc(cb_summed, 1)
                dve.wait_ge(setup_mm, 3)
                nc.vector.tensor_copy(w_u[:, :, :].rearrange("p c s -> p (c s)"), ps[:, 4, 0:FC * SD])\
                    .then_inc(setup_ev, 1)
                nc.vector.tensor_copy(cu[:, :], ps[0:SD, 5, 0:1]).then_inc(setup_ev, 1)
                nc.vector.tensor_scalar(mean[:, :], ps[0:SD, 6, 0:1], 1.0 / KEYS, None, ALU.mult)\
                    .then_inc(setup_ev, 1)
                dve.wait_ge(setup_mm, 4)
                nc.vector.tensor_tensor(c_aug[SD:SD + 1, :], ps[0:1, 7, :], bp, ALU.add)\
                    .then_inc(setup_ev, 1)

            def b_front(g, slot, loads, is_ctx):
                wait_apart(dve, xs_loaded[slot], 16 * loads, tick)
                layernorm(g, lambda t: xs[:, slot, t, :], lambda t: xs[:, slot, t, :], lambda: None, normed)

            def b_back(g, slot, *block_half):
                if isinstance(g, int) and g == 0:
                    setup()
                    return
                if isinstance(g, int) and g > CTX_G or block_half:
                    return
                for t in range(GT):
                    dve.wait_ge(v_done, GT * (g - 1) + (t + 1))
                    nc.vector.tensor_tensor(v[:, GT * (g - 1) + t, :], ps[:, 6 + t, :], bv, ALU.add)\
                        .then_inc(v_evac, 1)

            def own(hh):
                return slice(HD * hh, HD * hh + HD), slice(HD * (1 - hh), HD * (1 - hh) + HD)

            def q_low(v, hh):
                a, _ = own(hh)
                dve.wait_ge(q1_ready, v + 1)
                nc.vector.tensor_tensor(q2[0:HD, hh, :], qt_sb[a, :], q1[a, hh, :].bitcast(F32),
                                        ALU.subtract).then_inc(q2_ready, 1)

            def take_max(v, m):
                dve.wait_ge(max_done, NM * v + (m + 1))
                if m < NM - 1:
                    nc.vector.tensor_reduce(mx_part[:, m % QT_N, m // QT_N:m // QT_N + 1],
                                            ps[:, 4:6, :].rearrange("p a b -> p (a b)"), AX_X, ALU.max)\
                        .then_inc(max_taken, 1)
                else:
                    tails = ps[:, 4:6, 0:2 * (KEYS - TAIL)].rearrange("p b (q k) -> p b q k", q=2)
                    nc.vector.tensor_reduce(mx_part[:, :, 3].rearrange("p (b q) -> p b q", b=2), tails,
                                            AX_X, ALU.max).then_inc(max_taken, 1)

            def row_max(v, parts=mx_part):
                dve.wait_ge(max_taken, NM * v)
                nc.vector.tensor_reduce(mx[:, :], parts[:, :, :], AX_X, ALU.max).then_inc(max_ready, 1)

            def c_first(g):
                if g == CTX_G:
                    dve.wait_ge(kq_done, FC * CTX_G)
                    nc.vector.memset(q2[HD:HD + 2, :, :].bitcast(F32), 1.0).then_inc(q2_ones_set, 1)
                if g == CTX_G + 1:
                    dve.sem_inc(first_free, 1)
                if g == NG - 2:
                    dve.wait_ge(max_done, NM)
                    n = KEYS - TAIL
                    for b in (0, 1):
                        ins = nc.vector.tensor_reduce(mx_first[:, 2 * b:2 * b + 2, 6],
                                                      ps[:, 6 + b, 0:2 * n].rearrange("p (q k) -> p q k", q=2),
                                                      AX_X, ALU.max)
                    ins.then_inc(first_free, 1)
                    dve.wait_ge(first_free, NM + 1)
                    row_max(0, mx_first)

            def c_first_maxima(i, s):
                dve.wait_ge(max_done, 2 * i + (s + 1))
                nc.vector.tensor_reduce(mx_first[:, 2 * s:2 * s + 2, bass.ds(i, 1)], ps[:, 6:8, :], AX_X, ALU.max)\
                    .then_inc(first_free, 1)

            b_steps(dve, b_front, b_back, c_first, inside=c_first_maxima)

            def fold_sum(w):
                dve.wait_ge(summed_v, SUMS_V * w + (SUMS_V - 1))
                nc.vector.tensor_tensor(sums[:, 0, 0:QB], sums[:, 0, 0:QB], sums[:, 0, QB:], ALU.add)\
                    .then_inc(summed_v, 1)

            def add_pair(w, hh, s):
                dve.wait_ge(exped, NP * w + (s + 1))
                if s == 2:
                    wait(dve, summed_g, SUMS_G * w)
                    a = pt[:, pt_slot(hh, 0)]
                else:
                    dve.wait_ge(summed_v, SUMS_V * w + pe_sum_index(s))
                    a = sums[:, 0]
                nc.vector.tensor_tensor(sums[:, 0], a, pt[:, pt_slot(hh, s)], ALU.add).then_inc(summed_v, 1)

            for free in (o_even_free, o_odd_free):
                dve.sem_inc(free, 16)

            def scale_out(w, w_it, hh):
                dve.wait_ge(folded, w + 1)
                nc.vector.reciprocal(rden[:, :], ps[:, 7, QT_N * HD:QT_N * HD + QT_N]).then_inc(rden_ready, 1)
                dve.wait_ge(rden_ready, w + 1)
                wait(dve, (o_even_free, o_odd_free)[hh], 16 * (w_it + 1))
                nc.vector.tensor_tensor(o_out[:, hh], ps[:, 7, 0:QT_N * HD].rearrange("p (q d) -> p q d", q=QT_N),
                                        rden[:, :].rearrange("p (q o) -> p q o", o=1).to_broadcast([P, QT_N, HD]),
                                        ALU.mult).then_inc(o_scaled, 1)


            def c_unit(it, hh, first, last):
                w = 2 * it + hh
                w1, it1, hh1 = ahead(it, hh, 1)
                next1 = not (last and hh == 1)
                before = not (first and hh == 0)
                _, it_b, hh_b = ahead(it, hh, -1)
                for s in range(NP):
                    if s == NP - 1 and last and hh == 1:
                        dve.wait_ge(wo_hi_ready, 2)
                        for k in range(FC):
                            nc.vector.tensor_tensor(wo_lo[k], w_o[:, k], wo_hi[:, k].bitcast(F32), ALU.subtract)\
                                .then_inc(wo_lo_ready, 1)
                    if s == 0 and before:
                        add_pair(w - 1, hh_b, NP - 1)
                        fold_sum(w - 1)
                    if next1:
                        for m in MAX_AT[s][:1]:
                            take_max(w1, m)
                        if s == NP - 2:
                            row_max(w1)
                    if s == 2 and next1:
                        q_low(w1, hh1)
                    if s == 4 and before:
                        scale_out(w - 1, it_b, hh_b)
                    if s >= 3 and s % 2:
                        add_pair(w, hh, s - 1)
                    if next1:
                        for m in MAX_AT[s][1:]:
                            take_max(w1, m)

            c_steps(dve, c_unit)
            add_pair(UNIT_N - 1, 1, NP - 1)
            fold_sum(UNIT_N - 1)
            scale_out(UNIT_N - 1, ITERS - 1, 1)

            def project(d, slot, t):
                dve.wait_ge(xb_ready, d + 1)
                dve.wait_ge(y_done, GT * d + (t + 1))
                nc.vector.tensor_tensor(x1[:, GT * d + t, :], ps[:, 2 + t, :], xb[:, slot, t], ALU.add)\
                    .then_inc(x1_ready, 1)
                if t < GT - 1:
                    return
                wait_apart(dve, x1_ready, GT * (d + 1), tick)
                layernorm(d + NG, lambda t: x1[:, GT * d + t, :], lambda t: xn[:, t, :],
                          lambda: wait(dve, n2_turned, 2 * d), normed2)

            def nothing(d, slot):
                pass

            dve.wait_ge(scored, NP * UNIT_N)
            nc.vector.memset(c2[SD:MOD_LO + 1].bitcast(F32), 0.0)
            nc.vector.memset(s2[SD:MOD_LO + 1].bitcast(F32), 1.0).then_inc(c_cleared, 1)
            d_steps(dve, nothing, project, nothing, nothing)
            dve.wait_ge(c_hi, 1)
            nc.vector.tensor_tensor(c2[0:SD], c_aug[0:SD, :], c1[0:SD].bitcast(F32), ALU.subtract)
            nc.vector.tensor_tensor(c2[MOD_LO:MOD_LO + 1], c_aug[SD:SD + 1, :], c2[SD:SD + 1].bitcast(F32),
                                    ALU.subtract).then_inc(c_ready, 1)

            dve.wait_ge(u_ready, X_G)
            for h, c in scan_halves():
                nc.vector.memset(st[:, 0, c], 0.0).then_inc(st_ready, 1)

            with dve.Fori(0, LCH // 2) as i:
                for s in (0, 1):
                    for h, c in scan_halves():
                        dve.wait_ge(silu_done, 2 * (2 * i + s) + (h + 1))
                        nc.vector.tensor_tensor(st[:, 1 - s, c], sg[:, c], u_steps[:, 2 * i + s, c], ALU.add)\
                            .then_inc(st_ready, 1)
            dve.wait_ge(st_ready, 2 * (LCH + 1))
            nc.vector.tensor_copy(end1, st[:, 0]).then_inc(cmp_step, 1)
            nc.vector.memset(s_all[:, 0:1], 0.0)
            for h, c in scan_halves():
                a = max(c.start, 1)
                nc.vector.tensor_copy(s_from[:, 0, a:c.stop], st[:, 0, a - 1:c.stop - 1]).then_inc(st_ready, 1)
            with dve.Fori(0, LCH // 2) as i:
                for s in (0, 1):
                    for h, c in scan_halves():
                        dve.wait_ge(silu_done, 2 * (2 * i + (LCH + s)) + (h + 1))
                        nc.vector.tensor_tensor(s_to[:, 2 * i + s, c], sg[:, c], u_steps[:, 2 * i + s, c],
                                                ALU.add).then_inc(st_ready, 1)
            dve.wait_ge(st_ready, 2 * (2 * LCH + 2))
            ends = s_to[:, LCH - 1, :]
            nc.vector.tensor_tensor(diff, ends, end1, ALU.subtract).then_inc(cmp_step, 1)
            dve.wait_ge(cmp_step, 2)
            nc.vector.tensor_tensor(sq[:, 0], diff, diff, ALU.mult)
            nc.vector.tensor_tensor(sq[:, 1], ends, ends, ALU.mult).then_inc(cmp_step, 1)
            dve.wait_ge(sums_done, 1)
            nc.vector.tensor_copy(e_row, ps[0:1, 3, 0:NCH]).then_inc(cmp_step, 1)
            dve.wait_ge(cmp_step, 4)
            nc.vector.scalar_tensor_tensor(out=lhs_row, in0=e_row, scalar=-TOL2, in1=ps[0:1, 2, 0:NCH],
                                           op0=ALU.mult, op1=ALU.add).then_inc(cmp_step, 1)
            dve.wait_ge(cmp_step, 5)
            nc.vector.tensor_scalar(ok_row, lhs_row, 0.0, None, ALU.is_le).then_inc(cmp_step, 1)
            dve.wait_ge(cmp_step, 6)
            nc.vector.tensor_reduce(flag_f[:, 0:1], ok_row, AX_X, ALU.min).then_inc(cmp_step, 1)
            dve.wait_ge(cmp_step, 7)
            nc.vector.tensor_copy(flag[:, :], flag_f[:, 0:1]).then_inc(flag_ready, 1)
            dve.wait_ge(flag_ready, 1)
            good = dve.value_load(flag[0:1, 0:1], min_val=0, max_val=1)
            with dve.If(good == 0):
                with dve.Fori(0, T) as n:
                    dve.wait_ge(seq_silu, n + 1)
                    nc.vector.tensor_tensor(s_all[:, bass.ds(n + 1, 1)], sg[:, 0:1], u_all[:, bass.ds(n, 1)],
                                            ALU.add).then_inc(seq_st, 1)
                dve.wait_ge(seq_st, T)

            def f_add(d, slot):
                for t in range(GT):
                    dve.wait_ge(f_done, GT * d + (t + 1))
                    nc.vector.tensor_tensor(x1[:, GT * d + t, :], ps[:, 4 + 2 * slot + t, :],
                                            x1[:, GT * d + t, :], ALU.add).then_inc(f_added, 1)

            with dve.Fori(0, X_G // 2) as i:
                for s in (0, 1):
                    f_add(2 * i + s, s)

        @block.tensor
        def _(pe):
            mm = nc.tensor.matmul
            pe.wait_ge(consts, 6)

            def setup():
                pe.wait_ge(setup_loaded, 16 * 8)
                for m in range(FC):
                    for k in range(FC):
                        ins = mm(ps[:, 4, m * SD:(m + 1) * SD], win_sb[:, k, m * P:(m + 1) * P], b_sb[:, k, :],
                                 start=(k == 0), stop=(k == FC - 1))
                ins.then_inc(setup_mm, 1)
                for k in range(FC):
                    ins = mm(ps[0:SD, 5, 0:1], b_sb[:, k, :], bin_[:, k:k + 1], start=(k == 0), stop=(k == FC - 1))
                ins.then_inc(setup_mm, 1)
                pe.wait_ge(cb_summed, 1)
                mm(ps[0:SD, 6, 0:1], cb_sum, ones[:, :], start=True, stop=True).then_inc(setup_mm, 1)
                pe.wait_ge(setup_ev, 3)
                mm(ps[0:1, 7, :], mean[:, :], wp_sb, start=True, stop=True).then_inc(setup_mm, 1)
                pe.wait_ge(setup_ev, 4)

            def b_front(g, slot, loads, is_ctx):
                pe.wait_ge(normed, g + 1)
                wait(pe, nt_ready, FC * g)
                for c in range(FC):
                    for t in range(GT):
                        ins = nc.tensor.transpose(ps[:, c // 2, (c % 2) * GW + t * P:(c % 2) * GW + (t + 1) * P],
                                                  xs[:, slot, t, c * P:(c + 1) * P], ident[:, :])
                    if c % 2:
                        ins.then_inc(transposed, 1)

            def b_back(g, slot, *block_half):
                is_ctx = isinstance(g, int) and g < CTX_G or not isinstance(g, int) and not block_half
                if not is_ctx:
                    if isinstance(g, int) and g == CTX_G:
                        pe.wait_ge(w_loaded[0], 16)
                    pe.wait_ge(nt_ready, FC * (g + 1))
                    for c in range(FC):
                        wait(pe, kq_evac, FC * (g - 1) + (c + 1))
                        for k in range(FC):
                            ins = mm(ps[:, 2 + c, 0:GW], w3[:, 0, k, c * P:(c + 1) * P],
                                     nt[:, slot, k, :], start=(k == 0), stop=(k == FC - 1))
                        ins.then_inc(kq_done, 1)
                    return
                if isinstance(g, int) and g == 0:
                    setup()
                if isinstance(g, int) and g == 0:
                    pe.wait_ge(w_lo, 1)
                pe.wait_ge(n_lo, FC * (g + 1))
                passes = [(k, a, b) for k in range(FC) for a, b in ((0, 0), (0, 1), (1, 0))]
                for t in range(GT):
                    wait(pe, v_evac, GT * (g - 1) + (t + 1))
                    for n, (k, a, b) in enumerate(passes):
                        ins = mm(ps[:, 6 + t, :], n_part(slot, a, k)[:, t * P:(t + 1) * P],
                                 w_part(2, b)[:, k, :], start=(n == 0), stop=(n == len(passes) - 1))
                    ins.then_inc(v_done, 1)
                if isinstance(g, int) and g == 0:
                    pe.wait_ge(w_lo, 2)
                for c in range(FC):
                    wait(pe, kq_evac, FC * (g - 1) + (c + 1))
                    for n, (k, a, b) in enumerate(passes):
                        ins = mm(ps[:, 2 + c, 0:GW], w_part(1, a)[:, k, c * P:(c + 1) * P],
                                 n_part(slot, b, k), start=(n == 0), stop=(n == len(passes) - 1))
                    ins.then_inc(kq_done, 1)

            def maxima(v, hh, m):
                if m % QT_N == 0:
                    pe.wait_ge(k_lo, 4 * v + (m // QT_N + 1))
                if m == 0:
                    pe.wait_ge(qm_ready, v + 1)
                wait(pe, max_taken, NM * (v - 1) + m)
                if m < NM - 1:
                    a, q = 1024 * (m // QT_N), m % QT_N
                    for o in (0, 1):
                        ins = mm(ps[:, 4 + o, :], q_max[:, q * P:(q + 1) * P],
                                 k1[:, hh, a + 512 * o:a + 512 * (o + 1)], start=True, stop=True)
                else:
                    n = KEYS - TAIL
                    for q in range(QT_N):
                        ins = mm(ps[:, 4 + q // 2, (q % 2) * n:(q % 2 + 1) * n], q_max[:, q * P:(q + 1) * P],
                                 k1[:, hh, TAIL:KEYS], start=True, stop=True)
                ins.then_inc(max_done, 1)

            def turn_max(v):
                pe.wait_ge(max_ready, v + 1)
                wait(pe, o_scaled, v - 1)
                for q in range(QT_N):
                    ins = nc.tensor.transpose(ps[0:1, 7, q * P:(q + 1) * P], mx[:, q:q + 1], ident[:, :])
                ins.then_inc(max_turned, 1)

            def c_first(g):
                if g == CTX_G + 1:
                    pe.wait_ge(v_evac, GT * CTX_G)
                    pe.wait_ge(k_lo, 4)
                    pe.wait_ge(qm_ready, 1)
                if g == NG - 2:
                    pe.wait_ge(first_free, NM)
                    n = KEYS - TAIL
                    for q in range(QT_N):
                        ins = mm(ps[:, 6 + q // 2, (q % 2) * n:(q % 2 + 1) * n], q_max[:, q * P:(q + 1) * P],
                                 k1[:, 0, TAIL:KEYS], start=True, stop=True)
                    ins.then_inc(max_done, 1)
                if g == NG - 1:
                    turn_max(0)

            def c_first_maxima(i, s):
                pe.wait_ge(first_free, 2 * i + (s + 1))
                for q in (0, 1):
                    ins = mm(ps[:, 6 + q, :], q_max[:, (2 * s + q) * P:(2 * s + q + 1) * P],
                             k1[:, 0, bass.ds(512 * i, 512)], start=True, stop=True)
                ins.then_inc(max_done, 1)

            b_steps(pe, b_front, b_back, c_first, before=c_first_maxima)

            def scores(w, hh, s):
                for p, s_p in enumerate((0, 4, 8, 12)):
                    if s == s_p:
                        pe.wait_ge(k2_ready, 4 * w + (p + 1))
                if s == 0:
                    pe.wait_ge(q1_ready, w + 1)
                    pe.wait_ge(q2_ready, w + 1)
                    pe.wait_ge(shift_ready, w + 1)
                wait(pe, exped, NP * w + (s - 1))
                b = 2 * ((NP * hh + s) % 2)
                for i in (0, 1):
                    k = slice((2 * s + i) * P, (2 * s + i + 1) * P)
                    mm(ps[:, b + i, :], k1[:, hh, k], q1[:, hh, :], start=True, stop=False)
                    ins = mm(ps[:, b + i, :], k2[0:HD + 2, k], q2[0:HD + 2, hh, :], start=False, stop=True)
                ins.then_inc(scored, 1)

            def pv(w, w_it, hh, s):
                if s == 0:
                    pe.wait_ge((v_even_loaded, v_odd_loaded)[hh], 16 * (w_it + 1))
                    wait(pe, half_ready, w)
                pe.wait_ge(exped, NP * w + (s + 1))
                for i in (0, 1):
                    r = HD * i
                    ins = mm(ps[r:r + HD, 6, :], v_head[:, hh, 2 * s + i, :],
                             pt[:, pt_slot(hh, s), i * QB:(i + 1) * QB], start=(s == 0), stop=(s == NP - 1))
                ins.then_inc(pv_done, 1)

            def sum_out(w):
                pe.wait_ge(half_ready, w + 1)
                pe.wait_ge(summed_g, SUMS_G * (w + 1))
                wait(pe, o_scaled, w)
                for q in range(QT_N):
                    mm(ps[:, 7, QT_N * HD + q:QT_N * HD + q + 1], sums[:, 1, q * P:(q + 1) * P],
                       ones[:, :], start=True, stop=True)

            def fold_out(w):
                for q in range(QT_N):
                    ins = mm(ps[:, 7, q * HD:(q + 1) * HD], o_half[:, q * P:(q + 1) * P], fold[:, :],
                             start=True, stop=True)
                ins.then_inc(folded, 1)

            pe.wait_ge(kq_evac, FC * NG)
            pe.wait_ge(v_evac, GT * CTX_G)

            def c_unit(it, hh, first, last):
                w = 2 * it + hh
                w1, it1, hh1 = ahead(it, hh, 1)
                next1 = not (last and hh == 1)
                before = not (first and hh == 0)
                for s in range(NP):
                    scores(w, hh, s)
                    if s == NP - 1 and next1:
                        turn_max(w1)
                    if s == 0 and before:
                        pv(w - 1, ahead(it, hh, -1)[1], 1 - hh, NP - 1)
                    if s > 0:
                        pv(w, it, hh, s - 1)
                    if next1:
                        for m in MAX_AT[s][:1]:
                            maxima(w1, hh1, m)
                    if s == 3 and before:
                        sum_out(w - 1)
                        fold_out(w - 1)
                    if next1:
                        for m in MAX_AT[s][1:]:
                            maxima(w1, hh1, m)

            c_steps(pe, c_unit)
            pv(UNIT_N - 1, ITERS - 1, 1, NP - 1)
            sum_out(UNIT_N - 1)
            fold_out(UNIT_N - 1)

            def turn(d, slot):
                pe.wait_ge(og_loaded[slot], 8 * GT * (d - slot) + 16 * GT)
                wait(pe, ot_ready, 2 * d)
                for c in range(FC):
                    for t in range(GT):
                        ins = nc.tensor.transpose(ps[:, c // 2, (c % 2) * GW + t * P:(c % 2) * GW + (t + 1) * P],
                                                  og[:, slot, t, 2 * c:2 * c + 2].rearrange("p h d -> p (h d)"),
                                                  ident[:, :])
                    if c % 2:
                        ins.then_inc(o_turned, 1)

            def project(d, slot, t):
                pe.wait_ge(ot_lo_ready, 2 * (d + 1))
                wait(pe, x1_ready, GT * (d - 1) + (t + 1))
                for k in range(FC):
                    cols = slice(t * P, (t + 1) * P)
                    mm(ps[:, 2 + t, :], o_part(slot, 0, k)[:, cols], wo_hi[:, k], start=(k == 0), stop=False)
                    mm(ps[:, 2 + t, :], o_part(slot, 0, k)[:, cols], wo_lo[k], start=False, stop=False)
                    ins = mm(ps[:, 2 + t, :], o_part(slot, 1, k)[:, cols], wo_hi[:, k], start=False,
                             stop=(k == FC - 1))
                ins.then_inc(y_done, 1)

            def turn2(d, slot):
                pe.wait_ge(normed2, d + 1)
                wait(pe, n2t_ready, FC * d)
                for c in range(FC):
                    for t in range(GT):
                        ins = nc.tensor.transpose(
                            ps[:, 4 + c // 2, (c % 2) * GW + t * P:(c % 2) * GW + (t + 1) * P],
                            xn[:, t, c * P:(c + 1) * P], ident[:, :])
                    if c % 2:
                        ins.then_inc(n2_turned, 1)

            def finish(d, slot):
                pe.wait_ge(n2t_ready, FC * (d + 1))
                wait(pe, u_ready, d)
                for k in range(FC):
                    ins = mm(ps[0:SD, 6, 0:GW], w_u[:, k, :], nt[:, slot, k, :],
                             start=(k == 0), stop=(k == FC - 1))
                ins.then_inc(u_done, 1)

            pe.wait_ge(wo_lo_ready, FC)
            pe.wait_ge(o_scaled, UNIT_N)
            d_steps(pe, turn, project, turn2, finish)

            pe.wait_ge(at_loaded, 32)

            def scan_steps(first, states):
                with pe.Fori(0, LCH // 2) as i:
                    for s in (0, 1):
                        for h, c in scan_halves():
                            n = 2 * (2 * i + (first + s)) + (h + (3 if first else 1))
                            wait_apart(pe, st_ready, n, tick) if first else pe.wait_ge(st_ready, n)
                            mm(ps[:, h, 0:NCH // 2], at, states(i, s)[:, c], start=True, stop=True)\
                                .then_inc(z_done, 1)

            scan_steps(0, lambda i, s: st[:, s])
            scan_steps(LCH, lambda i, s: s_from[:, 2 * i + s])
            pe.wait_ge(cmp_step, 3)
            for k in (0, 1):
                ins = mm(ps[0:1, 2 + k, 0:NCH], ones[0:SD, :], sq[:, k], start=True, stop=True)
            ins.then_inc(sums_done, 1)
            pe.wait_ge(flag_ready, 1)
            good = pe.value_load(flag[0:1, 0:1], min_val=0, max_val=1)
            with pe.If(good == 0):
                mm(ps[:, 0, 0:1], at, s_all[:, 0:1], start=True, stop=True).then_inc(seq_z, 1)
                with pe.Fori(1, T) as n:
                    wait_apart(pe, seq_st, n, tick)
                    mm(ps[:, 0, 0:1], at, s_all[:, bass.ds(n, 1)], start=True, stop=True)\
                        .then_inc(seq_z, 1)

            def f_mm(d, slot):
                pe.wait_ge(s_lo, d + 1)
                for t in range(GT):
                    wait(pe, f_added, GT * (d - 2) + (t + 1))
                    b = 4 + 2 * slot + t
                    mm(ps[:, b, :], s1[:, slot, t * P:(t + 1) * P], c1, start=True, stop=False)
                    mm(ps[:, b, :], s2[:, slot, t * P:(t + 1) * P], c2, start=False, stop=True)\
                        .then_inc(f_done, 1)

            pe.wait_ge(c_ready, 1)
            for s in (0, 1):
                f_mm(s, s)
            with pe.Fori(1, X_G // 2) as i:
                for s in (0, 1):
                    f_mm(2 * i + s, s)


def kernel(**inputs):
    import numpy as np
    import concourse.bacc as bacc
    from concourse.bass_utils import run_bass_kernel_spmd

    g = {k.replace("L0_xattn_", ""): np.asarray(a) for k, a in inputs.items()}

    def column(a):
        return a.reshape(FC, P).T

    def padded(a):
        return np.concatenate([a, np.zeros((KPAD - KEYS, a.shape[1]), a.dtype)], axis=0)

    b_q, b_k, b_v = g["b_qkv"].reshape(3, H)
    arrays = {
        "x": g["x"].reshape(T, H),
        "ctx": padded(g["ctx_1024"].reshape(KEYS, H)),
        "ctxb": padded(g["ctxb_2048x64"].reshape(KEYS, SD)).reshape(KT_TILES, P, SD).transpose(1, 0, 2),
        "w_qkv_t": g["W_qkv"].reshape(3, H, FC, P).transpose(3, 0, 2, 1),
        "w_o_t": g["W_o"].reshape(H, FC, P).transpose(2, 1, 0),
        "w_in": g["W_in"].reshape(FC, P, H).transpose(1, 0, 2),
        "bmat": g["Bmat"].reshape(FC, P, SD).transpose(1, 0, 2),
        "w_prog_t": g["W_prog"].T,
        "a_t": g["A"].T,
        "cmat": g["Cmat"],
        "cols": np.stack([column(a) for a in (g["g1"], g["beta1"], g["g2"], g["beta2"], b_q, b_k, g["b_in"])],
                         axis=1),
        "bv_rows": np.broadcast_to(b_v, (P, H)),
        "bo_rows": np.broadcast_to(g["b_o"], (P, H)),
        "b_prog": g["b_prog"].reshape(1, H),
        "k2_rows": np.array([[1.0, 1.0], [0.0, PAD_SCORE]], np.float32),
    }
    arrays = {k: np.ascontiguousarray(a) for k, a in arrays.items()}
    nc = bacc.Bacc("TRN2", target_bir_lowering=False, num_devices=1)
    args = [nc.dram_tensor(k, list(a.shape), mybir.dt.from_np(a.dtype), kind="ExternalInput").ap()
            for k, a in arrays.items()]
    out = nc.dram_tensor("out", [T, H], F32, kind="ExternalOutput").ap()
    build(nc, *args, out)
    r = run_bass_kernel_spmd(nc, [arrays], core_ids=[0])
    return r.results[0]["out"].reshape(1, T, H)
```
